# Optimizing a Trainium2 kernel written in Bass

```python
import numpy as np
import jax
import jax.numpy as jnp

def _softmax(x, axis=-1):
    return jax.nn.softmax(x, axis=axis)

def _gelu(x):
    return jax.nn.gelu(x, approximate=True)

def _silu(x):
    return jax.nn.silu(x)

def _sigmoid(x):
    return jax.nn.sigmoid(x)

def _layernorm(x, axis=-1, eps=1e-05):
    m = jnp.mean(x, axis=axis, keepdims=True)
    v = jnp.var(x, axis=axis, keepdims=True)
    return (x - m) / jnp.sqrt(v + eps)

def _scatter_add(tgt, idx, src, axis=0):
    return tgt.at[idx].add(src)

def _segment_sum(src, seg, n):
    return jax.ops.segment_sum(src, seg, n)
kernel_name = 'mk_vit_tower_d1_tok_img1024_r4_af2d76'

def setup_inputs(seed: int=0):
    np.random.seed(seed)
    _w = jnp.asarray

    def _rec_inputs():
        import jax
        import jax.numpy as jnp
        _rk = jax.random.key(seed)
        x = -0.000125008 + 0.999885 * jax.random.normal(jax.random.fold_in(_rk, 1), (32, 4, 128, 256), jnp.float32)
        return x
    x = _rec_inputs()

    def _L0_tok_setup():
        import jax, jax.numpy as jnp
        import numpy as np
        key = jax.random.key(seed)
        k1, k2 = jax.random.split(key, 2)
        B, N, S, F = (16, 4, 128, 256)
        EMB = 256
        video_reps = jax.random.normal(k1, (B, N, S, F), dtype=jnp.float32)
        W = jax.random.normal(k2, (EMB, N * F), dtype=jnp.float32) * 0.02
        b = jnp.zeros((EMB,), dtype=jnp.float32)
        return {'video_reps': video_reps, 'W': W, 'b': b}
    _L0_tok_all = _L0_tok_setup()
    _L0_tok_in = {k: v for k, v in _L0_tok_all.items() if k in ('W', 'b')}
    del _L0_tok_all

    def _L0_attn_setup():
        import jax, jax.numpy as jnp
        import numpy as np
        D_MODEL = 256
        NUM_HEADS = 16
        D_K = D_MODEL // NUM_HEADS
        B, S = (4, 512)
        key = jax.random.key(seed)
        ks = jax.random.split(key, 9)
        s = 0.02
        return {'x': jax.random.normal(ks[0], (B, S, D_MODEL), dtype=jnp.float32), 'Wq': jax.random.normal(ks[1], (D_MODEL, D_MODEL), dtype=jnp.float32) * s, 'bq': jax.random.normal(ks[2], (D_MODEL,), dtype=jnp.float32) * s, 'Wk': jax.random.normal(ks[3], (D_MODEL, D_K), dtype=jnp.float32) * s, 'bk': jax.random.normal(ks[4], (D_K,), dtype=jnp.float32) * s, 'Wv': jax.random.normal(ks[5], (D_MODEL, D_K), dtype=jnp.float32) * s, 'bv': jax.random.normal(ks[6], (D_K,), dtype=jnp.float32) * s, 'Wo': jax.random.normal(ks[7], (D_MODEL, D_MODEL), dtype=jnp.float32) * s, 'bo': jax.random.normal(ks[8], (D_MODEL,), dtype=jnp.float32) * s}
    _L0_attn_all = _L0_attn_setup()
    _L0_attn_in = {k: v for k, v in _L0_attn_all.items() if k in ('Wq', 'bq', 'Wk', 'bk', 'Wv', 'bv', 'Wo', 'bo')}
    del _L0_attn_all

    def _L0_ffn_setup():
        import jax, jax.numpy as jnp
        import numpy as np
        D_MODEL = 256
        D_HIDDEN = 1024
        NUM_EXPERTS = 8
        B, T = (2, 512)
        key = jax.random.key(seed)
        ks = jax.random.split(key, 8)
        s = 0.02
        x = jax.random.normal(ks[0], (B, T, D_MODEL), dtype=jnp.float32)
        Wg = jax.random.normal(ks[1], (D_MODEL, NUM_EXPERTS), dtype=jnp.float32) * s
        bg = jnp.zeros((NUM_EXPERTS,), dtype=jnp.float32)
        W1 = jax.random.normal(ks[2], (NUM_EXPERTS, D_MODEL, D_HIDDEN), dtype=jnp.float32) * s
        b1 = jnp.zeros((NUM_EXPERTS, D_HIDDEN), dtype=jnp.float32)
        W2 = jax.random.normal(ks[3], (NUM_EXPERTS, D_HIDDEN, D_MODEL), dtype=jnp.float32) * s
        b2 = jnp.zeros((NUM_EXPERTS, D_MODEL), dtype=jnp.float32)
        return {'x': x, 'Wg': Wg, 'bg': bg, 'W1': W1, 'b1': b1, 'W2': W2, 'b2': b2}
    _L0_ffn_all = _L0_ffn_setup()
    _L0_ffn_in = {k: v for k, v in _L0_ffn_all.items() if k in ('Wg', 'bg', 'W1', 'b1', 'W2', 'b2')}
    del _L0_ffn_all
    return {'x': x, 'L0_tok_W': _L0_tok_in['W'], 'L0_tok_b': _L0_tok_in['b'], 'L0_attn_Wq': _L0_attn_in['Wq'], 'L0_attn_bq': _L0_attn_in['bq'], 'L0_attn_Wk': _L0_attn_in['Wk'], 'L0_attn_bk': _L0_attn_in['bk'], 'L0_attn_Wv': _L0_attn_in['Wv'], 'L0_attn_bv': _L0_attn_in['bv'], 'L0_attn_Wo': _L0_attn_in['Wo'], 'L0_attn_bo': _L0_attn_in['bo'], 'L0_ffn_Wg': _L0_ffn_in['Wg'], 'L0_ffn_bg': _L0_ffn_in['bg'], 'L0_ffn_W1': _L0_ffn_in['W1'], 'L0_ffn_b1': _L0_ffn_in['b1'], 'L0_ffn_W2': _L0_ffn_in['W2'], 'L0_ffn_b2': _L0_ffn_in['b2']}

def reference(x, L0_tok_W, L0_tok_b, L0_attn_Wq, L0_attn_bq, L0_attn_Wk, L0_attn_bk, L0_attn_Wv, L0_attn_bv, L0_attn_Wo, L0_attn_bo, L0_ffn_Wg, L0_ffn_bg, L0_ffn_W1, L0_ffn_b1, L0_ffn_W2, L0_ffn_b2):
    import jax
    import jax.numpy as jnp

    def _L0_tok_ref(video_reps, W, b):
        import jax, jax.numpy as jnp
        import numpy as np
        B, N, S, F = video_reps.shape
        base = video_reps[:, 0]
        others = video_reps[:, 1:]
        dots = jnp.einsum('bsf,bntf->bnst', base, others)
        n1 = jnp.linalg.norm(base, axis=-1)
        n2 = jnp.linalg.norm(others, axis=-1)
        sim = dots / n1[:, None, :, None] / n2[:, :, None, :]
        sim = jnp.nan_to_num(sim)
        aligned = jnp.einsum('bnst,bntf->bnsf', sim, others)
        feats = jnp.concatenate([base[:, None], aligned], axis=1)
        feats = jnp.moveaxis(feats, 1, 2).reshape(B, S, N * F)
        return feats @ W.T + b

    def _L0_attn_ref(x, Wq, bq, Wk, bk, Wv, bv, Wo, bo):
        import jax, jax.numpy as jnp
        import numpy as np
        D_MODEL = 256
        NUM_HEADS = 16
        D_K = D_MODEL // NUM_HEADS
        B, S = (4, 512)
        b, s, _ = x.shape
        Q = (x @ Wq + bq).reshape(b, s, NUM_HEADS, D_K)
        K = x @ Wk + bk
        V = x @ Wv + bv
        scale = 1.0 / jnp.sqrt(jnp.float32(D_K))
        scores = jnp.einsum('bqhd,bkd->bhqk', Q, K) * scale
        probs = jax.nn.softmax(scores, axis=-1)
        context = jnp.einsum('bhqk,bkd->bqhd', probs, V)
        context = context.reshape(b, s, D_MODEL)
        return context @ Wo + bo

    def _L0_ffn_ref(x, Wg, bg, W1, b1, W2, b2):
        import jax, jax.numpy as jnp
        import numpy as np
        D_MODEL = 256
        D_HIDDEN = 1024
        NUM_EXPERTS = 8
        B, T = (2, 512)
        gate_logits = jnp.einsum('btd,de->bte', x, Wg) + bg
        gate_scores = jax.nn.softmax(gate_logits, axis=-1)
        top1_idx = jnp.argmax(gate_scores, axis=-1)
        top1_mask = jax.nn.one_hot(top1_idx, NUM_EXPERTS, dtype=x.dtype)
        top1_weight = jnp.sum(gate_scores * top1_mask, axis=-1, keepdims=True)
        h = jax.nn.silu(jnp.einsum('btd,edh->bteh', x, W1) + b1)
        o = jnp.einsum('bteh,ehd->bted', h, W2) + b2
        y = jnp.sum(o * top1_mask[..., None], axis=2) * top1_weight
        return y
    h = _L0_tok_ref(x, L0_tok_W, L0_tok_b)
    h = h + _L0_attn_ref(_layernorm(h, axis=-1), L0_attn_Wq, L0_attn_bq, L0_attn_Wk, L0_attn_bk, L0_attn_Wv, L0_attn_bv, L0_attn_Wo, L0_attn_bo)
    h = h + _L0_ffn_ref(_layernorm(h, axis=-1), L0_ffn_Wg, L0_ffn_bg, L0_ffn_W1, L0_ffn_b1, L0_ffn_W2, L0_ffn_b2)
    return h

_drawn_inputs = setup_inputs


def setup_inputs(seed=0):
    import zlib

    import numpy as np

    out = dict(_drawn_inputs(seed))
    spreads = {'L0_tok_b': (0.0, 0.1),
     'L0_ffn_bg': (0.0, 0.32),
     'L0_ffn_b1': (0.0, 0.683),
     'L0_ffn_b2': (0.0, 0.1)}
    factors = {'L0_attn_Wq': 8.0,
     'L0_attn_bq': 8.0,
     'L0_attn_Wk': 8.0,
     'L0_attn_bk': 8.0,
     'L0_attn_bv': 4.735}
    for name, (base, spread) in spreads.items():
        noise = np.random.default_rng([zlib.crc32(name.encode()), seed]).standard_normal(out[name].shape)
        drawn = base * np.exp(spread * noise) if base else spread * noise
        out[name] = jnp.asarray(drawn.astype(out[name].dtype))
    for name, factor in factors.items():
        out[name] = (out[name] * factor).astype(out[name].dtype)
    return out
```

```python
from contextlib import ExitStack

import concourse.bass as bass
from concourse import mybir


def wait(eng, sem, value):
    if not isinstance(value, int) or value > 0:
        eng.wait_ge(sem, value)


def wait_alone(eng, sem, value):
    if not isinstance(value, int):
        eng.wait_ge(sem, value)
        eng.nop(nofuse=True)
    elif value > 0:
        eng.wait_ge(sem, value)


def visit(i, u, lag, count):
    item, use, buf = 2 * i + (u - lag), i + (u - lag) // 2, (u - lag) % 2
    if isinstance(i, int) and not 0 <= item < count:
        return None
    return item, use, buf


def at_most(value, limit):
    return min(value, limit) if isinstance(value, int) else value


def run_steps(eng, count, lag, step):
    lead = lag + 2 + lag % 2
    for j in range(lead):
        step(j // 2, j % 2)
    with eng.Fori(lead // 2, count // 2) as i:
        for u in range(2):
            step(i, u)
    for j in range(count // 2 * 2, count + lag):
        step(j // 2, j % 2)


def tower(nc, x, tok_W, tok_b, Wq, bq, Wk, bk, Wv, bv, Wo, bo, Wg, bg, W1, b1, W2, b2, out):
    fp32, bf16, i32 = mybir.dt.float32, mybir.dt.bfloat16, mybir.dt.int32
    fp32r = mybir.dt.float32r
    ALU, ACT, AX = mybir.AluOpType, mybir.ActivationFunctionType, mybir.AxisListType

    B, NV, P, F = x.shape
    E = tok_W.shape[0]
    DK = Wk.shape[1]
    HEADS = Wq.shape[1] // DK
    NE, _, HID = W1.shape
    KC = E // P
    HC = HID // P
    NO = NV - 1
    QKV = E + 2 * DK
    EPS = 1e-5
    TINY = 1e-37
    SCALE = DK ** -0.5
    TOKENS = B * P
    SUBS = 2
    SLOT_TOKENS = SUBS * P
    SLOTS = TOKENS // SLOT_TOKENS + NE - 1
    BLOCKS = SLOTS * SUBS
    FULL_SLOTS = TOKENS // SLOT_TOKENS
    TERMS = 6
    SROWS = TERMS * DK
    MPARTS = 2
    HB = HEADS // 4

    normed_rows = nc.dram_tensor("normed_rows", [TOKENS, E], fp32, kind="Internal").ap()
    residual_rows = nc.dram_tensor("residual_rows", [TOKENS, E], fp32, kind="Internal").ap()
    out_rows = out.rearrange("b s e -> (b s) e")

    ctx = ExitStack()
    with ctx:
        def sb(name, shape, dt=fp32):
            return ctx.enter_context(nc.sbuf_tensor(name, shape, dt))

        def pair(name, shape, dt=fp32):
            return [sb(f"{name}{k}", shape, dt) for k in range(2)]

        def sem(name):
            return ctx.enter_context(nc.semaphore(name))

        bank = [ctx.enter_context(nc.psum_tensor(f"bank{n}", [P, 512], fp32)) for n in range(4)]
        wide = ctx.enter_context(nc.psum_tensor("wide", [P, 4, 512], fp32))

        ident = sb("ident", [P, P])
        before = sb("before", [P, P])
        ones = sb("ones", [P, P])
        b1T = sb("b1T", [P, NE * HC])
        logits = sb("logits", [P, B, NE])
        row_id = sb("row_id", [P, BLOCKS], i32)
        row_weight = sb("row_weight", [P, BLOCKS])
        slot_expert = sb("slot_expert", [1, SLOTS], i32)
        front = ExitStack()
        def sbf(name, shape, dt=fp32):
            return front.enter_context(nc.sbuf_tensor(name, shape, dt))
        identb = sbf("identb", [P, P], bf16)
        minus_half = sbf("minus_half", [P, NV])
        tok_bias = sbf("tok_bias", [P, E])
        qkv_w = sbf("qkv_w", [P, KC, QKV])
        qkv_bias = sbf("qkv_bias", [P, QKV])
        wo_w = sbf("wo_w", [P, KC, E])
        wo_bias = sbf("wo_bias", [P, E])
        gate_w = sbf("gate_w", [P, KC, NE])
        gate_bias = sbf("gate_bias", [P, NE])
        w0T = sbf("w0T", [P, KC, E])
        STRIDE = [1, 3, 4]
        moving = [sbf(f"moving{k}", [P, KC, 9, P]) for k in range(2)]
        hb_all = sbf("hb_all", [P, B, E])
        qkv_all = sbf("qkv_all", [P, B, QKV])

        setup = sem("setup")
        gp_setup = sem("gp_setup")
        wT_ready, wT_copied = sem("wT_ready"), sem("wT_copied")
        const_done = sem("const_done")

        part1 = ExitStack()
        def sb1(name, shape, dt=fp32):
            return part1.enter_context(nc.sbuf_tensor(name, shape, dt))
        xin = [sb1(f"xin{k}", [P, NV, F]) for k in range(2)]
        xT = [sb1(f"xT{k}", [P, NO, KC, P]) for k in range(2)]
        square = [sb1(f"square{k}", [P, NV, F]) for k in range(2)]
        norms2 = [sb1(f"norms2{k}", [P, NV]) for k in range(2)]
        inv_norm = [sb1(f"inv_norm{k}", [P, NV]) for k in range(2)]
        simT = [sb1(f"simT{k}", [P, NO, P]) for k in range(2)]
        proj = [sb1(f"proj{k}", [P, NO, E]) for k in range(2)]
        base = [sb1(f"base{k}", [P, E]) for k in range(2)]
        h = [sb1(f"h{k}", [P, E]) for k in range(2)]
        bn = sb1("bn", [P, 6])
        mean_var = [sb1(f"mean_var{k}", [P, 2]) for k in range(2)]
        ln_scale = sb1("ln_scale", [P, 2])
        xn = [sb1(f"xn{k}", [P, E]) for k in range(2)]
        xnT = [sb1(f"xnT{k}", [P, KC, P]) for k in range(2)]
        w_in = sb1("w_in", [P, E // P, NV * F])
        b1_in = sb1("b1_in", [NE * HC, P])

        x_loaded = [sem(f"x_loaded{k}") for k in range(2)]
        xT_lo_ready, xT_hi_ready = sem("xT_lo_ready"), sem("xT_hi_ready")
        xT_lo_copied, xT_hi_copied = sem("xT_lo_copied"), sem("xT_hi_copied")
        squares_done, clamped, inv_norm_ready = sem("squares_done"), sem("clamped"), sem("inv_norm_ready")
        dots_ready, base_ready = sem("dots_ready"), sem("base_ready")
        simT_copied, proj_copied, base_copied = sem("simT_copied"), sem("proj_copied"), sem("base_copied")
        mix_ready, h_ready = sem("mix_ready"), sem("h_ready")
        bn_done, stats_ready = sem("bn_done"), sem("stats_ready")
        rstd1_done, shift1_done, xn_ready, hb_done = sem("rstd1_done"), sem("shift1_done"), sem("xn_ready"), sem("hb_done")
        xnT_ready, xnT_copied = sem("xnT_ready"), sem("xnT_copied")
        qkv_ready, qkv_stored = sem("qkv_ready"), sem("qkv_stored")

        lo, hi = bank[0], bank[1]
        base_ps, mix_ps = bank[2], bank[3]
        xn_ps = wide[:, 3, :]
        LAG1 = 3

        with nc.Block() as block:
            @block.sync
            def _(sp):
                sp.dma_start(w_in[:, :, :], tok_W.rearrange("(a p) n -> p a n", p=P)).then_inc(setup, 16)
                sp.dma_start(b1_in[:, :], b1.rearrange("e (c p) -> (e c) p", p=P)).then_inc(setup, 16)

                def step(i, u):
                    if v := visit(i, u, 0, B):
                        b, use, k = v
                        wait(sp, xT_hi_ready, b - 1)
                        wait(sp, squares_done, b - 1)
                        sp.dma_start(xin[k][:, :, :], x[b].rearrange("n s f -> s n f")).then_inc(x_loaded[k], 16)

                run_steps(sp, B, 0, step)

            @block.gpsimd
            def _(gp):
                gp.memset(ident[:, :], 0.0).then_inc(gp_setup, 1)
                gp.memset(identb[:, :], 0.0).then_inc(gp_setup, 1)
                gp.memset(ones[:, :], 1.0).then_inc(gp_setup, 1)
                gp.memset(minus_half[:, :], -0.5).then_inc(gp_setup, 1)
                gp.wait_ge(gp_setup, 4)
                for t in (ident, identb):
                    gp.affine_select(out=t[:, :], in_=t[:, :], compare_op=ALU.not_equal, fill=1.0,
                                     base=0, pattern=[[-1, P]], channel_multiplier=1).then_inc(gp_setup, 1)
                gp.affine_select(out=before[:, :], in_=ones[:, :], compare_op=ALU.is_gt, fill=0.0,
                                 base=0, pattern=[[1, P]], channel_multiplier=-1).then_inc(gp_setup, 1)
                for dst, src in ((tok_bias[:, :], tok_b), (qkv_bias[:, 0:E], bq), (qkv_bias[:, E:E + DK], bk),
                                 (qkv_bias[:, E + DK:], bv), (wo_bias[:, :], bo), (gate_bias[:, :], bg)):
                    gp.dma_start(dst, src.partition_broadcast(P)).then_inc(const_done, 16)
                chunks = "(c p) n -> p c n"
                for dst, src in ((qkv_w[:, :, 0:E], Wq), (qkv_w[:, :, E:E + DK], Wk), (qkv_w[:, :, E + DK:], Wv),
                                 (wo_w[:, :, :], Wo), (gate_w[:, :, :], Wg)):
                    gp.dma_start(dst, src.rearrange(chunks, p=P)).then_inc(const_done, 16)
                gp.wait_ge(const_done, 16 * 11)

                def step(i, u):
                    if v := visit(i, u, 2, B):
                        b, use, k = v
                        wait(gp, stats_ready, b + 1)
                        wait_alone(gp, xn_ready, b)
                        gp.tensor_scalar_add(ln_scale[:, 0:1], mean_var[k][:, 1:2], EPS).then_inc(rstd1_done, 1)
                        wait_alone(gp, rstd1_done, 2 * b + 1)
                        gp.tensor_tensor(ln_scale[:, 0:1], ln_scale[:, 0:1], minus_half[:, 0:1],
                                         ALU.pow).then_inc(rstd1_done, 1)
                        wait_alone(gp, rstd1_done, 2 * b + 2)
                        gp.tensor_scalar(ln_scale[:, 1:2], mean_var[k][:, 0:1], ln_scale[:, 0:1], -1.0,
                                         ALU.mult, ALU.mult).then_inc(shift1_done, 1)
                        wait(gp, shift1_done, b + 1)
                        wait_alone(gp, xnT_ready, b - 1)
                        gp.tensor_scalar(xn[k][:, :], h[k][:, :], ln_scale[:, 0:1], ln_scale[:, 1:2],
                                         ALU.mult, ALU.add).then_inc(xn_ready, 1)
                        gp.tensor_tensor(hb_all[:, b, :], h[k][:, :], wo_bias[:, :], ALU.add).then_inc(hb_done, 1)
                    if v := visit(i, u, 0, B):
                        b, use, k = v
                        wait(gp, squares_done, b + 1)
                        wait(gp, simT_copied, NO * (b - 1))
                        wait_alone(gp, h_ready, b - 1)
                        gp.tensor_scalar_max(norms2[k][:, :], norms2[k][:, :], TINY).then_inc(clamped, 1)
                        wait_alone(gp, clamped, b + 1)
                        gp.tensor_tensor(inv_norm[k][:, :], norms2[k][:, :], minus_half[:, :],
                                         ALU.pow).then_inc(inv_norm_ready, 1)

                run_steps(gp, B, LAG1, step)

            @block.tensor
            def _(pe):
                pe.wait_ge(setup, 32)
                pe.wait_ge(gp_setup, 7)
                for n in range(NV):
                    if n >= 2:
                        pe.wait_ge(wT_copied, n - 1)
                    for c in range(KC):
                        for a in range(E // P):
                            last = nc.tensor.transpose(bank[n % 2][:, (c * 2 + a) * P:(c * 2 + a + 1) * P],
                                                       w_in[:, a, n * F + c * P:n * F + (c + 1) * P], ident[:, :])
                    last.then_inc(wT_ready, 1)
                nc.tensor.transpose(bank[2][:, 0:NE * HC], b1_in[:, :],
                                    ident[0:NE * HC, 0:NE * HC]).then_inc(wT_ready, 1)
                pe.wait_ge(const_done, 16 * 11)
                pe.wait_ge(wT_copied, NV + 1)

                def step(i, u):
                    if v := visit(i, u, 0, B):
                        b, use, k = v
                        pe.wait_ge(x_loaded[k], 16 * use + 16)
                        for half, ps, ready, copied in ((0, lo, xT_lo_ready, xT_lo_copied),
                                                        (1, hi, xT_hi_ready, xT_hi_copied)):
                            wait(pe, copied, b)
                            for n in range(2):
                                for c in range(KC):
                                    last = nc.tensor.transpose(ps[:, (n * KC + c) * P:(n * KC + c + 1) * P],
                                                               xin[k][:, 2 * half + n, c * P:(c + 1) * P], ident[:, :])
                            last.then_inc(ready, 1)
                    if v := visit(i, u, 2, B):
                        b, use, k = v
                        wait(pe, simT_copied, NO * b + NO)
                        wait(pe, proj_copied, NO * b + NO)
                        wait(pe, h_ready, b)
                        for n in range(NO):
                            last = nc.tensor.matmul(mix_ps[:, 0:E], simT[k][:, n, :], proj[k][:, n, :],
                                                    start=(n == 0), stop=(n == NO - 1))
                        last.then_inc(mix_ready, 1)
                    if v := visit(i, u, 3, B):
                        b, use, k = v
                        wait(pe, xn_ready, b + 1)
                        wait(pe, qkv_stored, b)
                        for c in range(KC):
                            last = nc.tensor.transpose(xn_ps[:, c * P:(c + 1) * P], xn[k][:, c * P:(c + 1) * P],
                                                       ident[:, :])
                        last.then_inc(xnT_ready, 1)
                    if v := visit(i, u, 1, B):
                        b, use, k = v
                        wait(pe, xT_lo_copied, b + 1)
                        wait(pe, xT_hi_copied, b + 1)
                        for n in range(NO):
                            wait(pe, simT_copied, NO * (b - 1) + n + 1)
                            wait(pe, proj_copied, NO * (b - 1) + n + 1)
                            s = STRIDE[n]
                            for c in range(KC):
                                last = nc.tensor.matmul(wide[:, n, 0:3 * P], xT[k][:, n, c, :],
                                                        moving[k][:, c, 0:2 * s + 1:s, :],
                                                        start=(c == 0), stop=(c == KC - 1))
                            last.then_inc(dots_ready, 1)
                        wait(pe, base_copied, b)
                        for c in range(KC):
                            last = nc.tensor.matmul(base_ps[:, 0:E], moving[k][:, c, 0, :], w0T[:, c, :],
                                                    start=(c == 0), stop=(c == KC - 1))
                        last.then_inc(base_ready, 1)
                    if v := visit(i, u, 3, B):
                        b, use, k = v
                        wait(pe, xnT_copied, b + 1)
                        for c in range(KC):
                            last = nc.tensor.matmul(xn_ps[:, 0:QKV], xnT[k][:, c, :], qkv_w[:, c, :],
                                                    start=(c == 0), stop=(c == KC - 1))
                        last.then_inc(qkv_ready, 1)

                run_steps(pe, B, LAG1, step)

            @block.scalar
            def _(act):
                def step(i, u):
                    if v := visit(i, u, 0, B):
                        b, use, k = v
                        wait(act, xT_lo_ready, b + 1)
                        wait(act, base_ready, b - 1)
                        nc.scalar.copy(moving[k][:, :, 0, :], lo[:, 0:KC * P].rearrange("p (c s) -> p c s", c=KC))
                        nc.scalar.copy(xT[k][:, 0, :, :],
                                       lo[:, KC * P:2 * KC * P].rearrange("p (c s) -> p c s", c=KC)).then_inc(xT_lo_copied, 1)
                    if v := visit(i, u, 3, B):
                        b, use, k = v
                        wait(act, xnT_ready, b + 1)
                        wait(act, qkv_ready, b - 1)
                        nc.scalar.copy(xnT[k][:, :, :],
                                       xn_ps[:, 0:KC * P].rearrange("p (c s) -> p c s", c=KC)).then_inc(xnT_copied, 1)
                    if v := visit(i, u, 0, B):
                        b, use, k = v
                        act.wait_ge(x_loaded[k], 16 * use + 16)
                        wait(act, inv_norm_ready, b - 1)
                        for n in range(NV):
                            last = nc.scalar.activation(square[k][:, n, :], xin[k][:, n, :], ACT.Square,
                                                        accum_out=norms2[k][:, n:n + 1])
                        last.then_inc(squares_done, 1)
                    if v := visit(i, u, 1, B):
                        b, use, k = v
                        wait(act, inv_norm_ready, b + 1)
                        wait(act, mix_ready, b - 1)
                        for n in range(NO):
                            wait(act, dots_ready, NO * b + n + 1)
                            nc.scalar.activation(simT[k][:, n, :], wide[:, n, 0:P], ACT.Copy,
                                                 scale=inv_norm[k][:, n + 1:n + 2]).then_inc(simT_copied, 1)

                run_steps(act, B, LAG1, step)

            @block.vector
            def _(dve):
                for n in range(NV):
                    dve.wait_ge(wT_ready, n + 1)
                    src = bank[n % 2][:, :].rearrange("p (c a s) -> p c a s", c=KC, a=E // P)
                    if n == 0:
                        last = nc.vector.tensor_copy(w0T[:, :, :].rearrange("p c (a s) -> p c a s", s=P), src)
                    else:
                        s = STRIDE[n - 1]
                        for k in range(2):
                            last = nc.vector.tensor_copy(moving[k][:, :, s:2 * s + 1:s, :], src)
                    last.then_inc(wT_copied, 1)
                dve.wait_ge(wT_ready, NV + 1)
                nc.vector.tensor_copy(b1T[:, :], bank[2][:, 0:NE * HC]).then_inc(wT_copied, 1)
                dve.wait_ge(const_done, 16 * 11)

                def step(i, u):
                    if v := visit(i, u, 0, B):
                        b, use, k = v
                        wait(dve, xT_hi_ready, b + 1)
                        wait(dve, base_ready, b - 1)
                        nc.vector.tensor_copy(xT[k][:, 1:3, :, :],
                                              hi[:, :].rearrange("p (n c s) -> p n c s", n=2, c=KC)).then_inc(xT_hi_copied, 1)
                    if v := visit(i, u, 2, B):
                        b, use, k = v
                        wait(dve, mix_ready, b + 1)
                        wait(dve, base_copied, b + 1)
                        wait(dve, xn_ready, b - 1)
                        wait(dve, hb_done, b - 1)
                        nc.vector.scalar_tensor_tensor(out=h[k][:, :], in0=mix_ps[:, 0:E], scalar=inv_norm[k][:, 0:1],
                                                       in1=base[k][:, :], op0=ALU.mult, op1=ALU.add).then_inc(h_ready, 1)
                        wait(dve, h_ready, b + 1)
                        nc.vector.bn_stats(bn[:, :], h[k][:, :]).then_inc(bn_done, 1)
                        wait_alone(dve, bn_done, b + 1)
                        nc.vector.bn_aggr(mean_var[k][:, :], bn[:, :]).then_inc(stats_ready, 1)
                    if v := visit(i, u, 1, B):
                        b, use, k = v
                        wait(dve, mix_ready, b - 1)
                        for n in range(NO):
                            wait(dve, dots_ready, NO * b + n + 1)
                            wait(dve, simT_copied, NO * b + n + 1)
                            nc.vector.tensor_copy(proj[k][:, n, :], wide[:, n, P:3 * P]).then_inc(proj_copied, 1)
                        wait(dve, base_ready, b + 1)
                        nc.vector.tensor_tensor(base[k][:, :], base_ps[:, 0:E], tok_bias[:, :],
                                                ALU.add).then_inc(base_copied, 1)
                    if v := visit(i, u, 3, B):
                        b, use, k = v
                        wait(dve, qkv_ready, b + 1)
                        nc.vector.tensor_tensor(qkv_all[:, b, :], xn_ps[:, 0:QKV], qkv_bias[:, :],
                                                ALU.add).then_inc(qkv_stored, 1)

                run_steps(dve, B, LAG1, step)
        part1.close()

        part2 = ExitStack()
        def sb2(name, shape, dt=fp32):
            return [part2.enter_context(nc.sbuf_tensor(f"{name}{k}", shape, dt)) for k in range(2)]
        q_parts = sb2("q_parts", [P, HEADS, TERMS, DK], bf16)
        k_parts = sb2("k_parts", [P, TERMS, DK], bf16)
        q_rest = sb2("q_rest", [P, HEADS, DK])
        k_rest = sb2("k_rest", [P, DK])
        v_one = sb2("v_one", [P, 32])
        qT = sb2("qT", [SROWS + MPARTS, HEADS, P], bf16)
        kT = sb2("kT", [SROWS + MPARTS, P], bf16)
        neg_max = sb2("neg_max", [P, HEADS])
        max_parts = sb2("max_parts", [P, MPARTS, HEADS], bf16)
        max_T = sb2("max_T", [MPARTS * HEADS, P], bf16)
        probs = sb2("probs", [P, HEADS, P])
        pvT = sb2("pvT", [P, HB, P])
        inv_sum = sb2("inv_sum", [P, HEADS])
        context = sb2("context", [P, HEADS, DK])
        contextT = sb2("contextT", [P, KC, P])
        row = sb2("row", [P, 2, E])
        bn2 = sb2("bn2_", [P, 6])
        mv2 = sb2("mv2_", [P, 2])
        ln2 = sb2("ln2_", [P, 2])
        xn2T = sb2("xn2T", [P, KC, P])

        q1_ready, q_rest_ready, q2_ready = sem("q1_ready"), sem("q_rest_ready"), sem("q2_ready")
        q_ready, k_chain, k_ready, v_ready = sem("q_ready"), sem("k_chain"), sem("k_ready"), sem("v_ready")
        qT_ready, qT_copied, kT_ready, kT_copied = sem("qT_ready"), sem("qT_copied"), sem("kT_ready"), sem("kT_copied")
        s_ready, max_done, max_parts_ready = sem("s_ready"), sem("max_done"), sem("max_parts_ready")
        max1_done = sem("max1_done")
        maxT_ready, maxT_copied = sem("maxT_ready"), sem("maxT_copied")
        max_rows = [sem(f"max_rows{k}") for k in range(2)]
        sT_ready, exp_done, pv_ready, pvT_copied, pv_back, inv_sum_ready, context_ready = (
            sem("sT_ready"), sem("exp_done"), sem("pv_ready"), sem("pvT_copied"), sem("pv_back"), sem("inv_sum_ready"), sem("context_ready"))
        ctxT_ready, ctxT_copied, attn_ready, h2_ready = sem("ctxT_ready"), sem("ctxT_copied"), sem("attn_ready"), sem("h2_ready")
        bn2_done, stats2_ready, ln2_chain, xn2_ready = sem("bn2_done"), sem("stats2_ready"), sem("ln2_chain"), sem("xn2_ready")
        row_stored = [sem(f"row_stored{k}") for k in range(2)]
        xn2T_ready, xn2T_copied, gate_ready, gate_stored = sem("xn2T_ready"), sem("xn2T_copied"), sem("gate_ready"), sem("gate_stored")
        part2_const = sem("part2_const")

        q_ps = [bank[0][:, :].bitcast(bf16).rearrange("p (h s) -> p h s", s=P),
                bank[3][:, :].bitcast(bf16).rearrange("p (h s) -> p h s", s=P)]
        HH = HEADS // 2
        attn_ps, small_ps = bank[1], bank[2]
        small_bf = small_ps[:, :].bitcast(bf16)
        LAG2 = 5

        with nc.Block() as block:
            @block.sync
            def _(sp):
                def step(i, u):
                    if v := visit(i, u, 2, B):
                        b, use, k = v
                        wait(sp, maxT_copied, b + 1)
                        wait(sp, sT_ready, 2 * (b - 1))
                        for m in range(MPARTS):
                            sp.dma_start(qT[k][SROWS + m:SROWS + m + 1, :, :],
                                         max_T[k][m * HEADS:(m + 1) * HEADS, :]).then_inc(max_rows[k], 16)
                    if v := visit(i, u, 4, B):
                        b, use, k = v
                        wait(sp, h2_ready, b + 1)
                        sp.dma_start(residual_rows[bass.ds(b * P, P), :], row[k][:, 1, :]).then_inc(row_stored[k], 16)
                        wait(sp, xn2_ready, b + 1)
                        sp.dma_start(normed_rows[bass.ds(b * P, P), :], row[k][:, 0, :]).then_inc(row_stored[k], 16)

                run_steps(sp, B, LAG2, step)

            @block.gpsimd
            def _(gp):
                for k in range(2):
                    gp.memset(kT[k][SROWS:SROWS + MPARTS, :], 1.0).then_inc(part2_const, 1)
                    gp.wait_ge(part2_const, 3 * k + 1)
                    gp.memset(v_one[k][:, :], 0.0).then_inc(part2_const, 1)
                    gp.wait_ge(part2_const, 3 * k + 2)
                    gp.memset(v_one[k][:, DK:DK + 1], 1.0).then_inc(part2_const, 1)
                    gp.wait_ge(part2_const, 3 * k + 3)

                def step(i, u):
                    if v := visit(i, u, 0, B):
                        b, use, k = v
                        kb = qkv_all[:, b, E:E + DK]
                        k3 = lambda a, n: a.unsqueeze(1).broadcast_to([P, n, DK])
                        wait(gp, kT_ready, b - 1)
                        wait_alone(gp, k_ready, b - 1)
                        gp.tensor_copy(k_parts[k][:, 1:TERMS:2, :], k3(kb, 3)).then_inc(k_chain, 1)
                        wait_alone(gp, k_chain, 3 * b + 1)
                        gp.tensor_tensor(k_rest[k][:, :], kb, k_parts[k][:, 1, :], ALU.subtract).then_inc(k_chain, 1)
                        wait_alone(gp, k_chain, 3 * b + 2)
                        gp.tensor_copy(k_parts[k][:, 2:TERMS:2, :], k3(k_rest[k][:, :], 2)).then_inc(k_chain, 1)
                        wait_alone(gp, k_chain, 3 * b + 3)
                        gp.tensor_tensor(k_parts[k][:, 0, :], k_rest[k][:, :], k_parts[k][:, 2, :],
                                         ALU.subtract).then_inc(k_ready, 1)
                    if v := visit(i, u, 2, B):
                        b, use, k = v
                        wait_alone(gp, pv_ready, b - 1)
                        gp.tensor_copy(v_one[k][:, 0:DK], qkv_all[:, b, E + DK:]).then_inc(v_ready, 1)
                    if v := visit(i, u, 0, B):
                        b, use, k = v
                        qb = qkv_all[:, b, 0:E].rearrange("p (h d) -> p h d", d=DK)
                        wait(gp, q1_ready, b + 1)
                        wait_alone(gp, q_ready, b - 1)
                        gp.tensor_tensor(q_rest[k][:, :, :], qb, q_parts[k][:, :, 0, :], ALU.subtract).then_inc(q_rest_ready, 1)
                        wait_alone(gp, q2_ready, b + 1)
                        gp.tensor_tensor(q_parts[k][:, :, 5, :], q_rest[k][:, :, :], q_parts[k][:, :, 3, :],
                                         ALU.subtract).then_inc(q_ready, 1)
                    if v := visit(i, u, 4, B):
                        b, use, k = v
                        wait_alone(gp, stats2_ready, b + 1)
                        gp.tensor_scalar_add(ln2[k][:, 0:1], mv2[k][:, 1:2], EPS).then_inc(ln2_chain, 1)
                        wait_alone(gp, ln2_chain, 3 * b + 1)
                        gp.tensor_tensor(ln2[k][:, 0:1], ln2[k][:, 0:1], minus_half[:, 0:1],
                                         ALU.pow).then_inc(ln2_chain, 1)
                        wait_alone(gp, ln2_chain, 3 * b + 2)
                        gp.tensor_scalar(ln2[k][:, 1:2], mv2[k][:, 0:1], ln2[k][:, 0:1], -1.0,
                                         ALU.mult, ALU.mult).then_inc(ln2_chain, 1)
                        wait_alone(gp, ln2_chain, 3 * b + 3)
                        gp.tensor_scalar(row[k][:, 0, :], row[k][:, 1, :], ln2[k][:, 0:1], ln2[k][:, 1:2],
                                         ALU.mult, ALU.add).then_inc(xn2_ready, 1)

                run_steps(gp, B, LAG2, step)
                for k in range(2):
                    gp.wait_ge(row_stored[k], 32 * (B // 2))

            @block.tensor
            def _(pe):
                pe.wait_ge(part2_const, 6)

                def q_transposes(half, b, k):
                    wait(pe, q_ready, b + 1)
                    wait(pe, qT_copied, 2 * (b - 1) + half + 1)
                    for n in range(HH):
                        last = nc.tensor.transpose(q_ps[half][0:SROWS, n, :],
                                                   q_parts[k][:, half * HH + n, :, :].rearrange("p t d -> p (t d)"), identb[:, :])
                    last.then_inc(qT_ready, 1)

                def step(i, u):
                    if v := visit(i, u, 1, B):
                        b, use, k = v
                        q_transposes(0, b, k)
                    if v := visit(i, u, 4, B):
                        b, use, k = v
                        wait(pe, pvT_copied, b + 1)
                        for n in range(HB):
                            last = nc.tensor.transpose(attn_ps[:, n * P:(n + 1) * P], pvT[k][:, n, :], ident[:, :])
                        last.then_inc(pv_back, 1)
                    if v := visit(i, u, 1, B):
                        b, use, k = v
                        q_transposes(1, b, k)
                    if v := visit(i, u, 3, B):
                        b, use, k = v
                        pe.wait_ge(max_rows[k], 16 * MPARTS * (use + 1))
                        for n in range(4):
                            wait(pe, max_done, at_most(2 * (b + 1) + n // 2 + 1, 2 * B))
                            wait(pe, exp_done, 2 * (b - 1) + n // 2 + 1)
                            last = nc.tensor.matmul(wide[:, n, :], kT[k][:, :],
                                                    qT[k][:, n * HB:(n + 1) * HB, :].rearrange("r h s -> r (h s)"),
                                                    start=True, stop=True)
                            if n % 2:
                                last.then_inc(sT_ready, 1)
                    if v := visit(i, u, 1, B):
                        b, use, k = v
                        wait(pe, k_ready, b + 1)
                        wait(pe, gate_stored, b - 4)
                        wait(pe, maxT_copied, b - 1)
                        nc.tensor.transpose(small_bf[0:SROWS, 0:P], k_parts[k][:, :, :].rearrange("p t d -> p (t d)"),
                                            identb[:, :]).then_inc(kT_ready, 1)
                    if v := visit(i, u, 4, B):
                        b, use, k = v
                        wait(pe, context_ready, b + 1)
                        for c in range(KC):
                            last = nc.tensor.transpose(attn_ps[:, c * P:(c + 1) * P],
                                                       context[k][:, :, :].rearrange("p h d -> p (h d)")[:, c * P:(c + 1) * P],
                                                       ident[:, :])
                        last.then_inc(ctxT_ready, 1)
                    if v := visit(i, u, 2, B):
                        b, use, k = v
                        wait(pe, max_parts_ready, b + 1)
                        wait(pe, kT_copied, at_most(b + 2, B))
                        wait(pe, gate_stored, b - 3)
                        nc.tensor.transpose(small_bf[0:MPARTS * HEADS, 0:P],
                                            max_parts[k][:, :, :].rearrange("p m h -> p (m h)"),
                                            identb[:, :]).then_inc(maxT_ready, 1)
                    if v := visit(i, u, 4, B):
                        b, use, k = v
                        wait(pe, ctxT_copied, b + 1)
                        for c in range(KC):
                            last = nc.tensor.matmul(attn_ps[:, 0:E], contextT[k][:, c, :], wo_w[:, c, :],
                                                    start=(c == 0), stop=(c == KC - 1))
                        last.then_inc(attn_ready, 1)
                    if v := visit(i, u, 5, B):
                        b, use, k = v
                        wait(pe, xn2_ready, b + 1)
                        wait(pe, maxT_copied, at_most(b + 4, B))
                        wait(pe, kT_copied, at_most(b + 5, B))
                        wait(pe, gate_stored, b)
                        for c in range(KC):
                            last = nc.tensor.transpose(small_ps[:, c * P:(c + 1) * P], row[k][:, 0, c * P:(c + 1) * P],
                                                       ident[:, :])
                        last.then_inc(xn2T_ready, 1)
                    if v := visit(i, u, 1, B):
                        b, use, k = v
                        wait(pe, qT_copied, 2 * b + 2)
                        wait(pe, kT_copied, b + 1)
                        for n in range(4):
                            wait(pe, exp_done, 2 * (b - 2) + n // 2 + 1)
                            for hh in range(HB):
                                last = nc.tensor.matmul(wide[:, n, hh * P:(hh + 1) * P], qT[k][0:SROWS, n * HB + hh, :],
                                                        kT[k][0:SROWS, :], start=True, stop=True)
                            if n % 2:
                                last.then_inc(s_ready, 1)
                    if v := visit(i, u, 5, B):
                        b, use, k = v
                        wait(pe, xn2T_copied, b + 1)
                        for c in range(KC):
                            last = nc.tensor.matmul(small_ps[:, 0:NE], xn2T[k][:, c, :], gate_w[:, c, :],
                                                    start=(c == 0), stop=(c == KC - 1))
                        last.then_inc(gate_ready, 1)
                    if v := visit(i, u, 3, B):
                        b, use, k = v
                        wait(pe, exp_done, 2 * b + 2)
                        wait(pe, v_ready, b + 1)
                        wait(pe, h2_ready, b)
                        for n in range(4):
                            last = nc.tensor.matmul(attn_ps[32 * n:32 * (n + 1), :], v_one[k][:, :],
                                                    probs[k][:, n * HB:(n + 1) * HB, :].rearrange("p h s -> p (h s)"),
                                                    start=True, stop=True)
                        last.then_inc(pv_ready, 1)

                run_steps(pe, B, LAG2, step)

            @block.scalar
            def _(act):
                nc.scalar.preload_act_table(ACT.Exp)

                def exp_half(n, b, k):
                    wait(act, sT_ready, 2 * b + n + 1)
                    wait(act, pv_ready, b - 1)
                    nc.scalar.activation(probs[k][:, n * HH:(n + 1) * HH, :],
                                         wide[:, 2 * n:2 * n + 2, :].rearrange("p a (h s) -> p (a h) s", s=P),
                                         ACT.Exp, scale=SCALE).then_inc(exp_done, 1)

                def step(i, u):
                    if v := visit(i, u, 0, B):
                        b, use, k = v
                        wait(act, qT_ready, 2 * (b - 1))
                        nc.scalar.copy(q_parts[k][:, :, 0:3, :],
                                       qkv_all[:, b, 0:E].rearrange("p (h d) -> p h d", d=DK)
                                       .unsqueeze(2).broadcast_to([P, HEADS, 3, DK])).then_inc(q1_ready, 1)
                    if v := visit(i, u, 3, B):
                        b, use, k = v
                        exp_half(0, b, k)
                    if v := visit(i, u, 4, B):
                        b, use, k = v
                        wait(act, ctxT_ready, b + 1)
                        wait(act, attn_ready, b - 1)
                        nc.scalar.copy(contextT[k][:, :, :],
                                       attn_ps[:, 0:KC * P].rearrange("p (c s) -> p c s", c=KC)).then_inc(ctxT_copied, 1)
                    if v := visit(i, u, 2, B):
                        b, use, k = v
                        wait(act, maxT_ready, b + 1)
                        if not isinstance(use, int) or use > 0:
                            act.wait_ge(max_rows[k], 16 * MPARTS * use)
                        nc.scalar.copy(max_T[k][:, :], small_bf[0:MPARTS * HEADS, 0:P]).then_inc(maxT_copied, 1)
                    if v := visit(i, u, 0, B):
                        b, use, k = v
                        wait(act, q_rest_ready, b + 1)
                        nc.scalar.copy(q_parts[k][:, :, 3:5, :],
                                       q_rest[k][:, :, :].unsqueeze(2).broadcast_to([P, HEADS, 2, DK])).then_inc(q2_ready, 1)
                    if v := visit(i, u, 3, B):
                        b, use, k = v
                        exp_half(1, b, k)
                    if v := visit(i, u, 5, B):
                        b, use, k = v
                        wait(act, xn2T_ready, b + 1)
                        wait(act, gate_ready, b - 1)
                        nc.scalar.copy(xn2T[k][:, :, :],
                                       small_ps[:, 0:KC * P].rearrange("p (c s) -> p c s", c=KC)).then_inc(xn2T_copied, 1)
                    if v := visit(i, u, 3, B):
                        b, use, k = v
                        wait(act, pv_ready, b + 1)
                        wait(act, pv_back, b - 1)
                        nc.scalar.copy(pvT[k][:, :, :], attn_ps[:, :].rearrange("p (h s) -> p h s", s=P)).then_inc(pvT_copied, 1)

                run_steps(act, B, LAG2, step)

            @block.vector
            def _(dve):
                def q_copy(half, b, k):
                    wait(dve, qT_ready, 2 * b + half + 1)
                    wait(dve, sT_ready, 2 * (b - 1))
                    nc.vector.tensor_copy(qT[k][0:SROWS, half * HH:(half + 1) * HH, :],
                                          q_ps[half][0:SROWS, :, :]).then_inc(qT_copied, 1)

                def step(i, u):
                    if v := visit(i, u, 4, B):
                        b, use, k = v
                        pv = attn_ps[:, :].rearrange("p (n j d) -> p j n d", n=HB, j=4)
                        wait(dve, pv_back, b + 1)
                        wait(dve, ctxT_ready, b - 1)
                        nc.vector.reciprocal(inv_sum[k][:, :].rearrange("p (j n) -> p j n", j=4),
                                             pv[:, :, :, DK]).then_inc(inv_sum_ready, 1)
                        wait(dve, inv_sum_ready, b + 1)
                        nc.vector.tensor_tensor(context[k][:, :, :].rearrange("p (j n) d -> p j n d", j=4), pv[:, :, :, 0:DK],
                                                inv_sum[k][:, :].rearrange("p (j n) -> p j n", j=4)
                                                .unsqueeze(3).broadcast_to([P, 4, HB, DK]),
                                                ALU.mult).then_inc(context_ready, 1)
                    if v := visit(i, u, 1, B):
                        b, use, k = v
                        wait(dve, kT_ready, b + 1)
                        wait(dve, sT_ready, 2 * (b - 1))
                        nc.vector.tensor_copy(kT[k][0:SROWS, :], small_bf[0:SROWS, 0:P]).then_inc(kT_copied, 1)
                    if v := visit(i, u, 1, B):
                        b, use, k = v
                        q_copy(0, b, k)
                    if v := visit(i, u, 1, B):
                        b, use, k = v
                        q_copy(1, b, k)
                    if v := visit(i, u, 4, B):
                        b, use, k = v
                        wait(dve, attn_ready, b + 1)
                        if not isinstance(use, int) or use > 0:
                            dve.wait_ge(row_stored[k], 32 * use)
                        wait(dve, xn2T_ready, b - 1)
                        nc.vector.tensor_tensor(row[k][:, 1, :], attn_ps[:, 0:E], hb_all[:, b, :],
                                                ALU.add).then_inc(h2_ready, 1)
                        wait(dve, h2_ready, b + 1)
                        nc.vector.bn_stats(bn2[k][:, :], row[k][:, 1, :]).then_inc(bn2_done, 1)
                        wait(dve, bn2_done, b + 1)
                        wait_alone(dve, xn2_ready, b - 1)
                        nc.vector.bn_aggr(mv2[k][:, :], bn2[k][:, :]).then_inc(stats2_ready, 1)
                    if v := visit(i, u, 1, B):
                        b, use, k = v
                        for n in range(2):
                            wait(dve, s_ready, 2 * b + n + 1)
                            wait(dve, max_parts_ready, b - 1)
                            nc.vector.tensor_reduce(out=neg_max[k][:, n * HH:(n + 1) * HH],
                                                    in_=wide[:, 2 * n:2 * n + 2, :].rearrange("p a (h s) -> p (a h) s", s=P),
                                                    axis=AX.X, op=ALU.max, negate=True).then_inc(max_done, 1)
                        wait(dve, max_done, 2 * b + 2)
                        wait(dve, maxT_ready, b - 1)
                        nc.vector.tensor_copy(max_parts[k][:, 0, :], neg_max[k][:, :]).then_inc(max1_done, 1)
                        wait(dve, max1_done, b + 1)
                        nc.vector.tensor_tensor(max_parts[k][:, 1, :], neg_max[k][:, :], max_parts[k][:, 0, :],
                                                ALU.subtract).then_inc(max_parts_ready, 1)
                    if v := visit(i, u, 5, B):
                        b, use, k = v
                        wait(dve, gate_ready, b + 1)
                        nc.vector.tensor_tensor(logits[:, b, :], small_ps[:, 0:NE], gate_bias[:, :],
                                                ALU.add).then_inc(gate_stored, 1)

                run_steps(dve, B, LAG2, step)
        part2.close()

        routing = ExitStack()
        def sbr(name, shape, dt=fp32):
            return routing.enter_context(nc.sbuf_tensor(name, shape, dt))

        token = sbr("token", [P, B])
        expert_rank = sbr("expert_rank", [P, NE])
        slot_fill = sbr("slot_fill", [P, FULL_SLOTS])
        block_no = sbr("block_no", [P, BLOCKS])
        lane_no = sbr("lane_no", [P, P])
        slot_no = sbr("slot_no", [P, SLOTS])
        best = sbr("best", [P, B])
        below = sbr("below", [P, B, NE])
        expd = sbr("expd", [P, B, NE])
        total = sbr("total", [P, B])
        weight = sbr("weight", [P, B])
        is_best = sbr("is_best", [P, B, NE])
        chosen = sbr("chosen", [P, B])
        onehot = sbr("onehot", [P, B, NE])
        counts = sbr("counts", [P, NE, B])
        running = sbr("running", [P, NE, B])
        earlier = sbr("earlier", [P, NE, B])
        n_tokens = sbr("n_tokens", [P, NE])
        more_than = sbr("more_than", [P, NE, FULL_SLOTS])
        n_slots = sbr("n_slots", [P, NE])
        slot_end = sbr("slot_end", [P, NE])
        first_row = sbr("first_row", [P, NE])
        place = sbr("place", [P, B, NE])
        picked = sbr("picked", [P, B, NE])
        position = sbr("position", [P, B])
        position_i = sbr("position_i", [P, B], i32)
        block_i = sbr("block_i", [P, B], i32)
        lane_i = sbr("lane_i", [P, B], i32)
        block_f = sbr("block_f", [P, B])
        lane_f = sbr("lane_f", [P, B])
        in_lane = sbr("in_lane", [P, B, P])
        in_block = sbr("in_block", [P, B, 2, BLOCKS])
        padding = sbr("padding", [P, BLOCKS])
        row_id_f = sbr("row_id_f", [P, BLOCKS])
        past = sbr("past", [1, SLOTS, NE])
        slot_expert_f = sbr("slot_expert_f", [1, SLOTS])

        iotas, r_chain, exp_ready = sem("iotas"), sem("r_chain"), sem("exp_ready")
        below_ready, onehot_ready, ranks_ready = sem("below_ready"), sem("onehot_ready"), sem("ranks_ready")
        lanes_ready, table_ready = sem("lanes_ready"), sem("table_ready")
        rank_ps, count_ps, table_ps = bank[0], bank[1], bank[2]
        GROUPS = 4
        GB = B // GROUPS

        with nc.Block() as block:
            @block.gpsimd
            def _(gp):
                gp.iota(token[:, :], pattern=[[P, B]], base=1, channel_multiplier=1,
                        allow_small_or_imprecise_dtypes=True).then_inc(iotas, 1)
                gp.iota(expert_rank[:, :], pattern=[[-1, NE]], base=NE, channel_multiplier=0,
                        allow_small_or_imprecise_dtypes=True).then_inc(iotas, 1)
                gp.iota(slot_fill[:, :], pattern=[[SLOT_TOKENS, FULL_SLOTS]], base=0, channel_multiplier=0,
                        allow_small_or_imprecise_dtypes=True).then_inc(iotas, 1)
                gp.iota(block_no[:, :], pattern=[[1, BLOCKS]], base=0, channel_multiplier=0,
                        allow_small_or_imprecise_dtypes=True).then_inc(iotas, 1)
                gp.iota(lane_no[:, :], pattern=[[1, P]], base=0, channel_multiplier=0,
                        allow_small_or_imprecise_dtypes=True).then_inc(iotas, 1)
                gp.iota(slot_no[:, :], pattern=[[1, SLOTS]], base=0, channel_multiplier=0,
                        allow_small_or_imprecise_dtypes=True).then_inc(iotas, 1)

            @block.scalar
            def _(act):
                act.wait_ge(below_ready, 1)
                nc.scalar.activation(expd[:, :, :], below[:, :, :], ACT.Exp).then_inc(exp_ready, 1)

            @block.tensor
            def _(pe):
                flat = onehot[:, :, :].rearrange("p b e -> p (b e)")
                pe.wait_ge(onehot_ready, 1)
                nc.tensor.matmul(rank_ps[:, 0:B * NE], before[:, :], flat, start=True, stop=True)
                nc.tensor.matmul(count_ps[:, 0:B * NE], ones[:, :], flat, start=True, stop=True).then_inc(ranks_ready, 1)
                for b in range(B):
                    if b % GB == 0:
                        pe.wait_ge(lanes_ready, b // GB + 1)
                    last = nc.tensor.matmul(table_ps[:, 0:2 * BLOCKS], in_lane[:, b, :],
                                            in_block[:, b, :, :].rearrange("p a n -> p (a n)"),
                                            start=(b == 0), stop=(b == B - 1))
                last.then_inc(table_ready, 1)

            @block.vector
            def _(dve):
                done = [0]

                def after(ins):
                    done[0] += 1
                    ins.then_inc(r_chain, 1)
                    dve.wait_ge(r_chain, done[0])

                def by_expert(a):
                    return a.unsqueeze(2).broadcast_to([P, B, NE])

                dve.wait_ge(iotas, 6)
                after(nc.vector.tensor_reduce(out=best[:, :], in_=logits[:, :, :], axis=AX.X, op=ALU.max))
                nc.vector.tensor_tensor(below[:, :, :], logits[:, :, :], by_expert(best[:, :]),
                                        ALU.subtract).then_inc(below_ready, 1)
                dve.wait_ge(below_ready, 1)
                after(nc.vector.tensor_scalar(is_best[:, :, :], below[:, :, :], 0.0, None, ALU.is_ge))
                after(nc.vector.tensor_tensor(is_best[:, :, :], is_best[:, :, :],
                                              expert_rank[:, :].unsqueeze(1).broadcast_to([P, B, NE]), ALU.mult))
                after(nc.vector.tensor_reduce(out=chosen[:, :], in_=is_best[:, :, :], axis=AX.X, op=ALU.max))
                nc.vector.tensor_tensor(onehot[:, :, :], by_expert(chosen[:, :]),
                                        expert_rank[:, :].unsqueeze(1).broadcast_to([P, B, NE]),
                                        ALU.is_equal).then_inc(onehot_ready, 1)
                dve.wait_ge(exp_ready, 1)
                after(nc.vector.tensor_reduce(out=total[:, :], in_=expd[:, :, :], axis=AX.X, op=ALU.add))
                after(nc.vector.reciprocal(weight[:, :], total[:, :]))
                dve.wait_ge(ranks_ready, 1)
                after(nc.vector.tensor_copy(counts[:, :, :], count_ps[:, 0:B * NE].rearrange("p (b e) -> p e b", e=NE)))
                flat = "p e b -> p (e b)"
                after(nc.vector.tensor_tensor_scan(out=running[:, :, :].rearrange(flat), data0=ones[:, 0:1].broadcast_to([P, NE * B]),
                                                   data1=counts[:, :, :].rearrange(flat), initial=0.0,
                                                   op0=ALU.mult, op1=ALU.add))
                after(nc.vector.tensor_tensor(earlier[:, :, :], running[:, :, :], counts[:, :, :], ALU.subtract))
                after(nc.vector.tensor_tensor(n_tokens[:, :], running[:, :, B - 1], earlier[:, :, 0], ALU.subtract))
                after(nc.vector.tensor_tensor(more_than[:, :, :], n_tokens[:, :].unsqueeze(2).broadcast_to([P, NE, FULL_SLOTS]),
                                              slot_fill[:, :].unsqueeze(1).broadcast_to([P, NE, FULL_SLOTS]), ALU.is_gt))
                after(nc.vector.tensor_reduce(out=n_slots[:, :], in_=more_than[:, :, :], axis=AX.X, op=ALU.add))
                after(nc.vector.tensor_tensor_scan(out=slot_end[:, :], data0=ones[:, 0:NE], data1=n_slots[:, :],
                                                   initial=0.0, op0=ALU.mult, op1=ALU.add))
                after(nc.vector.tensor_tensor(first_row[:, :], slot_end[:, :], n_slots[:, :], ALU.subtract))
                after(nc.vector.scalar_tensor_tensor(out=first_row[:, :], in0=first_row[:, :], scalar=float(SLOT_TOKENS),
                                                     in1=earlier[:, :, 0], op0=ALU.mult, op1=ALU.subtract))
                after(nc.vector.tensor_tensor(place[:, :, :], rank_ps[:, 0:B * NE].rearrange("p (b e) -> p b e", e=NE),
                                              earlier[:, :, :].rearrange("p e b -> p b e"), ALU.add))
                after(nc.vector.tensor_tensor(place[:, :, :], place[:, :, :],
                                              first_row[:, :].unsqueeze(1).broadcast_to([P, B, NE]), ALU.add))
                after(nc.vector.tensor_tensor(picked[:, :, :], place[:, :, :], onehot[:, :, :], ALU.mult))
                after(nc.vector.tensor_reduce(out=position[:, :], in_=picked[:, :, :], axis=AX.X, op=ALU.add))
                after(nc.vector.tensor_copy(position_i[:, :], position[:, :]))
                after(nc.vector.tensor_scalar(block_i[:, :], position_i[:, :], P.bit_length() - 1, None,
                                              ALU.logical_shift_right))
                after(nc.vector.tensor_scalar(lane_i[:, :], position_i[:, :], P - 1, None, ALU.bitwise_and))
                after(nc.vector.tensor_copy(block_f[:, :], block_i[:, :]))
                after(nc.vector.tensor_copy(lane_f[:, :], lane_i[:, :]))
                for g in range(GROUPS):
                    s = slice(g * GB, (g + 1) * GB)
                    wide_shape = [P, GB, BLOCKS]
                    after(nc.vector.tensor_tensor(in_block[:, s, 0, :], block_no[:, :].unsqueeze(1).broadcast_to(wide_shape),
                                                  block_f[:, s].unsqueeze(2).broadcast_to(wide_shape), ALU.is_equal))
                    after(nc.vector.tensor_tensor(in_block[:, s, 1, :], in_block[:, s, 0, :],
                                                  weight[:, s].unsqueeze(2).broadcast_to(wide_shape), ALU.mult))
                    after(nc.vector.tensor_tensor(in_block[:, s, 0, :], in_block[:, s, 0, :],
                                                  token[:, s].unsqueeze(2).broadcast_to(wide_shape), ALU.mult))
                    nc.vector.tensor_tensor(in_lane[:, s, :], lane_no[:, :].unsqueeze(1).broadcast_to([P, GB, P]),
                                            lane_f[:, s].unsqueeze(2).broadcast_to([P, GB, P]),
                                            ALU.is_equal).then_inc(lanes_ready, 1)
                after(nc.vector.tensor_tensor(past[:, :, :], slot_no[0:1, :].unsqueeze(2).broadcast_to([1, SLOTS, NE]),
                                              slot_end[0:1, :].unsqueeze(1).broadcast_to([1, SLOTS, NE]), ALU.is_ge))
                after(nc.vector.tensor_reduce(out=slot_expert_f[:, :], in_=past[:, :, :], axis=AX.X, op=ALU.add))
                after(nc.vector.tensor_scalar_min(slot_expert_f[:, :], slot_expert_f[:, :], float(NE - 1)))
                after(nc.vector.tensor_copy(slot_expert[:, :], slot_expert_f[:, :]))
                dve.wait_ge(table_ready, 1)
                nc.vector.tensor_copy(row_weight[:, :], table_ps[:, BLOCKS:2 * BLOCKS])
                after(nc.vector.tensor_scalar(padding[:, :], table_ps[:, 0:BLOCKS], 0.5, float(2 * TOKENS),
                                              ALU.is_lt, ALU.mult))
                after(nc.vector.scalar_tensor_tensor(out=row_id_f[:, :], in0=table_ps[:, 0:BLOCKS], scalar=-1.0,
                                                     in1=padding[:, :], op0=ALU.add, op1=ALU.add))
                after(nc.vector.tensor_copy(row_id[:, :], row_id_f[:, :]))
        routing.close()

        front.close()
        w1_in = pair("w1_in", [P, KC, HID])
        w1_hi, w1_lo = pair("w1_hi", [P, KC, HID], fp32r), pair("w1_lo", [P, KC, HID], fp32r)
        w2_in = pair("w2_in", [P, HC, E])
        w2_hi, w2_lo = pair("w2_hi", [P, HC, E], fp32r), pair("w2_lo", [P, HC, E], fp32r)
        b2_rows = pair("b2_rows", [P, E])
        b1_cols = pair("b1_cols", [P, HC])
        gather_ids = [pair(f"gather_ids{m}_", [P, 1], i32) for m in range(SUBS)]
        scatter_ids = [pair(f"scatter_ids{m}_", [P, 1], i32) for m in range(SUBS)]
        weights = pair("weights", [P, SUBS])
        normed = [pair(f"normed{m}_", [P, E]) for m in range(SUBS)]
        residual = [pair(f"residual{m}_", [P, E]) for m in range(SUBS)]
        slotT_hi, slotT_lo = pair("slotT_hi", [P, KC, SLOT_TOKENS], fp32r), pair("slotT_lo", [P, KC, SLOT_TOKENS], fp32r)
        hidden = pair("hidden", [P, HC, SLOT_TOKENS])
        hidden_hi, hidden_lo = pair("hidden_hi", [P, HC, SLOT_TOKENS], fp32r), pair("hidden_lo", [P, HC, SLOT_TOKENS], fp32r)
        plus_b2 = [pair(f"plus_b2_{m}_", [P, E]) for m in range(SUBS)]
        finished = [pair(f"finished{m}_", [P, E]) for m in range(SUBS)]

        w1_loaded = [sem(f"w1_loaded{k}") for k in range(2)]
        w2_loaded = [sem(f"w2_loaded{k}") for k in range(2)]
        b2_loaded = [sem(f"b2_loaded{k}") for k in range(2)]
        normed_in = [[sem(f"normed_in{m}_{k}") for k in range(2)] for m in range(SUBS)]
        residual_in = [[sem(f"residual_in{m}_{k}") for k in range(2)] for m in range(SUBS)]
        scattered = [[sem(f"scattered{m}_{k}") for k in range(2)] for m in range(SUBS)]
        w1_hi_ready, w1_lo_ready = sem("w1_hi_ready"), sem("w1_lo_ready")
        w2_hi_ready, w2_lo_ready = sem("w2_hi_ready"), sem("w2_lo_ready")
        rows_cleared, gather_ids_ready, scatter_ids_ready = sem("rows_cleared"), sem("gather_ids_ready"), sem("scatter_ids_ready")
        slotT_ready, slotT_hi_ready, slotT_lo_ready = sem("slotT_ready"), sem("slotT_hi_ready"), sem("slotT_lo_ready")
        picks_ready, up_ready, down_ready = sem("picks_ready"), sem("up_ready"), sem("down_ready")
        silu_done, hidden_hi_ready, hidden_lo_ready = sem("silu_done"), sem("hidden_hi_ready"), sem("hidden_lo_ready")
        plus_b2_ready, finished_ready = sem("plus_b2_ready"), sem("finished_ready")
        slot_ps, down_ps = bank[0], [bank[1], bank[2]]
        PAIRS = HC // 2
        W2_PARTS = 2
        W2_C = HC // W2_PARTS
        W1_N = HID * KC // PAIRS
        LAG3 = 2

        def split_products(acc, a_hi, a_lo, b_hi, b_lo, first, last):
            nc.tensor.matmul(acc, a_hi, b_hi, start=first, stop=False)
            nc.tensor.matmul(acc, a_hi, b_lo, start=False, stop=False)
            return nc.tensor.matmul(acc, a_lo, b_hi, start=False, stop=last)

        with nc.Block() as block:
            @block.sync
            def _(sp):
                def step(i, u):
                    if v := visit(i, u, 0, SLOTS):
                        s, use, k = v
                        e = sp.value_load(slot_expert[0:1, bass.ds(s, 1)], min_val=0, max_val=NE - 1)
                        wait(sp, w1_lo_ready, PAIRS * (s - 1))
                        sp.dma_start(w1_in[k][:, :, :], W1[e].rearrange("(c p) n -> p c n", p=P)).then_inc(w1_loaded[k], 16)
                        wait(sp, w2_lo_ready, W2_PARTS * (s - 1))
                        sp.dma_start(w2_in[k][:, :, :], W2[e].rearrange("(c p) n -> p c n", p=P)).then_inc(w2_loaded[k], 16)
                    if v := visit(i, u, 1, SLOTS):
                        s, use, k = v
                        e = sp.value_load(slot_expert[0:1, bass.ds(s, 1)], min_val=0, max_val=NE - 1)
                        wait(sp, plus_b2_ready, SUBS * (s - 1))
                        sp.dma_start(b2_rows[k][:, :], b2[e].partition_broadcast(P)).then_inc(b2_loaded[k], 16)

                run_steps(sp, SLOTS, 1, step)

            @block.gpsimd
            def _(gp):
                for k in range(2):
                    for m in range(SUBS):
                        gp.memset(normed[m][k][:, :], 0.0).then_inc(rows_cleared, 1)
                        gp.memset(residual[m][k][:, :], 0.0).then_inc(rows_cleared, 1)
                gp.wait_ge(rows_cleared, 2 * 2 * SUBS)

                def gather(dst, table, ids_):
                    return gp.indirect_dma_start(out=dst, out_offset=None, in_=table,
                                                 in_offset=bass.IndirectOffsetOnAxis(ap=ids_[:, 0:1], axis=0),
                                                 bounds_check=TOKENS - 1, oob_is_err=False)

                def step(i, u):
                    if v := visit(i, u, 0, SLOTS):
                        s, use, k = v
                        wait_alone(gp, slotT_ready, s - 1)
                        for m in range(SUBS):
                            if not isinstance(use, int) or use > 0:
                                wait_alone(gp, residual_in[m][k], 16 * use)
                            gp.tensor_copy(gather_ids[m][k][:, :], row_id[:, bass.ds(SUBS * s + m, 1)]).then_inc(gather_ids_ready, 1)
                            wait_alone(gp, gather_ids_ready, SUBS * s + m + 1)
                            gather(normed[m][k][:, :], normed_rows, gather_ids[m][k]).then_inc(normed_in[m][k], 16)
                    for m in range(SUBS):
                        if v := visit(i, u, 2, SLOTS):
                            s, use, k = v
                            if not isinstance(use, int) or use > 0:
                                wait_alone(gp, scattered[m][k], 16 * use)
                            gp.tensor_copy(scatter_ids[m][k][:, :], row_id[:, bass.ds(SUBS * s + m, 1)]).then_inc(scatter_ids_ready, 1)
                            wait_alone(gp, finished_ready, SUBS * s + m + 1)
                            wait_alone(gp, scatter_ids_ready, SUBS * s + m + 1)
                            gp.indirect_dma_start(out=out_rows, in_=finished[m][k][:, :], in_offset=None,
                                                  out_offset=bass.IndirectOffsetOnAxis(ap=scatter_ids[m][k][:, 0:1], axis=0),
                                                  bounds_check=TOKENS - 1, oob_is_err=False).then_inc(scattered[m][k], 16)

                        if v := visit(i, u, 0, SLOTS):
                            s, use, k = v
                            wait_alone(gp, finished_ready, SUBS * (s - 2) + m + 1)
                            gather(residual[m][k][:, :], residual_rows, gather_ids[m][k]).then_inc(residual_in[m][k], 16)

                run_steps(gp, SLOTS, LAG3, step)
                for k in range(2):
                    for m in range(SUBS):
                        gp.wait_ge(scattered[m][k], 16 * ((SLOTS + 1 - k) // 2))

            @block.tensor
            def _(pe):
                def down(s, k, m, chunks):
                    if chunks[0] == 0:
                        wait(pe, plus_b2_ready, SUBS * (s - 1) + m + 1)
                    for c in chunks:
                        if m == 0 and c % 2 == 0:
                            wait(pe, hidden_lo_ready, PAIRS * s + c // 2 + 1)
                        block_m = slice(m * P, (m + 1) * P)
                        last = split_products(down_ps[m][:, 0:E], hidden_hi[k][:, c, block_m], hidden_lo[k][:, c, block_m],
                                              w2_hi[k][:, c, :], w2_lo[k][:, c, :], c == 0, c == HC - 1)
                    if c == HC - 1:
                        last.then_inc(down_ready, 1)

                def step(i, u):
                    if v := visit(i, u, 2, SLOTS):
                        s, use, k = v
                        wait(pe, slotT_lo_ready, s + 1)
                        wait(pe, w1_lo_ready, PAIRS * (s + 1))
                        for c in range(HC):
                            if c % 2 == 0:
                                wait(pe, silu_done, PAIRS * (s - 1) + c // 2 + 1)
                            for kc in range(KC):
                                chunk = slice(c * P, (c + 1) * P)
                                last = split_products(wide[:, c // 2, (c % 2) * SLOT_TOKENS:(c % 2 + 1) * SLOT_TOKENS],
                                                      w1_hi[k][:, kc, chunk], w1_lo[k][:, kc, chunk],
                                                      slotT_hi[k][:, kc, :], slotT_lo[k][:, kc, :], kc == 0, kc == KC - 1)
                            if c % 2:
                                last.then_inc(up_ready, 1)
                        wait(pe, w2_lo_ready, W2_PARTS * (s + 1))
                        down(s, k, 0, range(0, HC - 2))
                        down(s, k, 1, range(0, HC // 2))
                    if v := visit(i, u, 1, SLOTS):
                        s, use, k = v
                        wait(pe, slotT_lo_ready, s)
                        for m in range(SUBS):
                            pe.wait_ge(normed_in[m][k], 16 * use + 16)
                            for c in range(KC):
                                last = nc.tensor.transpose(slot_ps[:, c * SLOT_TOKENS + m * P:c * SLOT_TOKENS + (m + 1) * P],
                                                           normed[m][k][:, c * P:(c + 1) * P], ident[:, :])
                        last.then_inc(slotT_ready, 1)
                    if v := visit(i, u, 2, SLOTS):
                        s, use, k = v
                        down(s, k, 0, range(HC - 2, HC))
                        down(s, k, 1, range(HC // 2, HC))

                run_steps(pe, SLOTS, LAG3, step)

            @block.scalar
            def _(act):
                nc.scalar.preload_act_table(ACT.Silu)

                def step(i, u):
                    if v := visit(i, u, 2, SLOTS):
                        s, use, k = v
                        wait(act, picks_ready, s + 1)
                        wait(act, hidden_lo_ready, PAIRS * (s - 1))
                        wait(act, down_ready, SUBS * (s - 1))
                        for p in range(PAIRS):
                            wait(act, up_ready, PAIRS * s + p + 1)
                            for c in (2 * p, 2 * p + 1):
                                last = nc.scalar.activation(hidden[k][:, c, :],
                                                            wide[:, p, (c % 2) * SLOT_TOKENS:(c % 2 + 1) * SLOT_TOKENS],
                                                            ACT.Silu, bias=b1_cols[k][:, c:c + 1])
                            last.then_inc(silu_done, 1)
                            wait(act, silu_done, PAIRS * s + p + 1)
                            nc.scalar.copy(hidden_hi[k][:, 2 * p:2 * p + 2, :],
                                           hidden[k][:, 2 * p:2 * p + 2, :]).then_inc(hidden_hi_ready, 1)
                    if v := visit(i, u, 1, SLOTS):
                        s, use, k = v
                        act.wait_ge(w2_loaded[k], 16 * use + 16)
                        wait(act, down_ready, SUBS * (s - 1))
                        nc.scalar.copy(w2_hi[k][:, :, :], w2_in[k][:, :, :]).then_inc(w2_hi_ready, 1)
                    if v := visit(i, u, 0, SLOTS):
                        s, use, k = v
                        act.wait_ge(w1_loaded[k], 16 * use + 16)
                        wait(act, up_ready, PAIRS * (s - 1))
                        nc.scalar.copy(w1_hi[k][:, :, :], w1_in[k][:, :, :]).then_inc(w1_hi_ready, 1)

                run_steps(act, SLOTS, LAG3, step)

            @block.vector
            def _(dve):
                def low_part(dst, src, hi_part):
                    return nc.vector.tensor_tensor(dst, src, hi_part.bitcast(fp32), ALU.subtract)

                def finish(s, use, k, m):
                    wait(dve, down_ready, SUBS * s + m + 1)
                    nc.vector.tensor_tensor(plus_b2[m][k][:, :], down_ps[m][:, 0:E], b2_rows[k][:, :],
                                            ALU.add).then_inc(plus_b2_ready, 1)
                    wait(dve, plus_b2_ready, SUBS * s + m + 1)
                    dve.wait_ge(residual_in[m][k], 16 * use + 16)
                    if not isinstance(use, int) or use > 0:
                        dve.wait_ge(scattered[m][k], 16 * use)
                    nc.vector.scalar_tensor_tensor(out=finished[m][k][:, :], in0=plus_b2[m][k][:, :],
                                                   scalar=weights[k][:, m:m + 1], in1=residual[m][k][:, :],
                                                   op0=ALU.mult, op1=ALU.add).then_inc(finished_ready, 1)

                def w2_low(s, k, part):
                    cs = slice(part * W2_C, (part + 1) * W2_C)
                    low_part(w2_lo[k][:, cs, :], w2_in[k][:, cs, :], w2_hi[k][:, cs, :]).then_inc(w2_lo_ready, 1)

                def step(i, u):
                    current, following = visit(i, u, 2, SLOTS), visit(i, u, 1, SLOTS)
                    for p in range(PAIRS):
                        if current:
                            s, use, k = current
                            wait(dve, hidden_hi_ready, PAIRS * s + p + 1)
                            wait(dve, down_ready, SUBS * (s - 1))
                            low_part(hidden_lo[k][:, 2 * p:2 * p + 2, :], hidden[k][:, 2 * p:2 * p + 2, :],
                                     hidden_hi[k][:, 2 * p:2 * p + 2, :]).then_inc(hidden_lo_ready, 1)
                        if following:
                            s, use, k = following
                            wait(dve, w1_hi_ready, s + 1)
                            wait(dve, up_ready, PAIRS * (s - 1))
                            kc, n = divmod(p * W1_N, HID)
                            low_part(w1_lo[k][:, kc, n:n + W1_N], w1_in[k][:, kc, n:n + W1_N],
                                     w1_hi[k][:, kc, n:n + W1_N]).then_inc(w1_lo_ready, 1)
                    if following:
                        s, use, k = following
                        e = dve.value_load(slot_expert[0:1, bass.ds(s, 1)], min_val=0, max_val=NE - 1)
                        wait(dve, silu_done, PAIRS * (s - 1))
                        wait(dve, finished_ready, SUBS * (s - 1))
                        nc.vector.tensor_copy(b1_cols[k][:, :], b1T[:, bass.ds(e * HC, HC)])
                        nc.vector.tensor_copy(weights[k][:, :], row_weight[:, bass.ds(SUBS * s, SUBS)]).then_inc(picks_ready, 1)
                        wait(dve, slotT_ready, s + 1)
                        wait(dve, up_ready, PAIRS * (s - 1))
                        by_chunk = slot_ps[:, :].rearrange("p (c s) -> p c s", c=KC)
                        nc.vector.tensor_copy(slotT_hi[k][:, :, :], by_chunk).then_inc(slotT_hi_ready, 1)
                        wait(dve, slotT_hi_ready, s + 1)
                        low_part(slotT_lo[k][:, :, :], by_chunk, slotT_hi[k][:, :, :]).then_inc(slotT_lo_ready, 1)
                    if current:
                        s, use, k = current
                        wait(dve, picks_ready, s + 1)
                        dve.wait_ge(b2_loaded[k], 16 * use + 16)
                        finish(s, use, k, 0)
                    if following:
                        s, use, k = following
                        wait(dve, w2_hi_ready, s + 1)
                        wait(dve, down_ready, SUBS * (s - 1))
                        w2_low(s, k, 0)
                    if current:
                        s, use, k = current
                        finish(s, use, k, 1)
                    if following:
                        s, use, k = following
                        w2_low(s, k, 1)

                run_steps(dve, SLOTS, LAG3, step)


_INS = ["x", "L0_tok_W", "L0_tok_b", "L0_attn_Wq", "L0_attn_bq", "L0_attn_Wk", "L0_attn_bk", "L0_attn_Wv",
        "L0_attn_bv", "L0_attn_Wo", "L0_attn_bo", "L0_ffn_Wg", "L0_ffn_bg", "L0_ffn_W1", "L0_ffn_b1",
        "L0_ffn_W2", "L0_ffn_b2"]


def kernel(**inputs):
    import numpy as np
    import concourse.bacc as bacc
    from concourse.bass_utils import run_bass_kernel_spmd

    nc = bacc.Bacc("TRN2", target_bir_lowering=False, num_devices=1)
    arrays, args = {}, []
    for name in _INS:
        a = np.ascontiguousarray(inputs[name])
        arrays[f"in_{name}"] = a
        args.append(nc.dram_tensor(f"in_{name}", a.shape, mybir.dt.from_np(a.dtype), kind="ExternalInput").ap())
    batch, _, tokens, _ = arrays["in_x"].shape
    embed = arrays["in_L0_tok_W"].shape[0]
    out = nc.dram_tensor("out", (batch, tokens, embed), mybir.dt.float32, kind="ExternalOutput").ap()
    tower(nc, *args, out)
    return run_bass_kernel_spmd(nc, [arrays], core_ids=[0]).results[0]["out"]
```

```python
from contextlib import ExitStack

import concourse.bass as bass
from concourse import mybir


def wait(eng, sem, value):
    if not isinstance(value, int) or value > 0:
        eng.wait_ge(sem, value)


def wait_alone(eng, sem, value):
    if not isinstance(value, int):
        eng.wait_ge(sem, value)
        eng.nop(nofuse=True)
    elif value > 0:
        eng.wait_ge(sem, value)


def visit(i, u, lag, count):
    item, use, buf = 2 * i + (u - lag), i + (u - lag) // 2, (u - lag) % 2
    if isinstance(i, int) and not 0 <= item < count:
        return None
    return item, use, buf


def at_most(value, limit):
    return min(value, limit) if isinstance(value, int) else value


def run_steps(eng, count, lag, step):
    lead = lag + 2 + lag % 2
    for j in range(lead):
        step(j // 2, j % 2)
    with eng.Fori(lead // 2, count // 2) as i:
        for u in range(2):
            step(i, u)
    for j in range(count // 2 * 2, count + lag):
        step(j // 2, j % 2)


def tower(nc, x, tok_W, tok_b, Wq, bq, Wk, bk, Wv, bv, Wo, bo, Wg, bg, W1, b1, W2, b2, out):
    fp32, bf16, i32 = mybir.dt.float32, mybir.dt.bfloat16, mybir.dt.int32
    fp32r = mybir.dt.float32r
    ALU, ACT, AX = mybir.AluOpType, mybir.ActivationFunctionType, mybir.AxisListType

    B, NV, P, F = x.shape
    E = tok_W.shape[0]
    DK = Wk.shape[1]
    HEADS = Wq.shape[1] // DK
    NE, _, HID = W1.shape
    KC = E // P
    HC = HID // P
    NO = NV - 1
    QKV = E + 2 * DK
    EPS = 1e-5
    TINY = 1e-37
    SCALE = DK ** -0.5
    TOKENS = B * P
    SUBS = 2
    SLOT_TOKENS = SUBS * P
    SLOTS = TOKENS // SLOT_TOKENS + NE - 1
    BLOCKS = SLOTS * SUBS
    FULL_SLOTS = TOKENS // SLOT_TOKENS
    TERMS = 6
    SROWS = TERMS * DK
    MPARTS = 2
    HB = HEADS // 4

    normed_rows = nc.dram_tensor("normed_rows", [TOKENS, E], fp32, kind="Internal").ap()
    residual_rows = nc.dram_tensor("residual_rows", [TOKENS, E], fp32, kind="Internal").ap()
    out_rows = out.rearrange("b s e -> (b s) e")

    ctx = ExitStack()
    with ctx:
        def sb(name, shape, dt=fp32):
            return ctx.enter_context(nc.sbuf_tensor(name, shape, dt))

        def pair(name, shape, dt=fp32):
            return [sb(f"{name}{k}", shape, dt) for k in range(2)]

        def sem(name):
            return ctx.enter_context(nc.semaphore(name))

        bank = [ctx.enter_context(nc.psum_tensor(f"bank{n}", [P, 512], fp32)) for n in range(4)]
        wide = ctx.enter_context(nc.psum_tensor("wide", [P, 4, 512], fp32))

        ident = sb("ident", [P, P])
        before = sb("before", [P, P], bf16)
        ones = sb("ones", [P, P], bf16)
        b1T = sb("b1T", [P, NE * HC])
        logits = sb("logits", [P, B, NE])
        row_id = sb("row_id", [P, BLOCKS], i32)
        row_weight = sb("row_weight", [P, BLOCKS])
        slot_expert = sb("slot_expert", [1, SLOTS], i32)
        front = ExitStack()
        def sbf(name, shape, dt=fp32):
            return front.enter_context(nc.sbuf_tensor(name, shape, dt))
        identb = sbf("identb", [P, P], bf16)
        minus_half = sbf("minus_half", [P, NV])
        tok_bias = sbf("tok_bias", [P, E])
        qkv_w = sbf("qkv_w", [P, KC, QKV])
        qkv_w_hi, qkv_w_lo = sbf("qkv_w_hi", [P, KC, QKV], fp32r), sbf("qkv_w_lo", [P, KC, QKV], fp32r)
        qkv_bias = sbf("qkv_bias", [P, QKV])
        wo_w = sbf("wo_w", [P, KC, E])
        wo_bias = sbf("wo_bias", [P, E])
        gate_w = sbf("gate_w", [P, KC, NE])
        gate_bias = sbf("gate_bias", [P, NE])
        w0T_hi, w0T_lo = sbf("w0T_hi", [P, KC, E], fp32r), sbf("w0T_lo", [P, KC, E], fp32r)
        STRIDE = [1, 3, 4]
        moving_hi = [sbf(f"moving_hi{k}", [P, KC, 9, P], fp32r) for k in range(2)]
        moving_lo = [sbf(f"moving_lo{k}", [P, KC, 9, P], fp32r) for k in range(2)]
        hb_all = sbf("hb_all", [P, B, E])
        qkv_all = sbf("qkv_all", [P, B, QKV])

        def low_part(dst, src, hi_part):
            return nc.vector.tensor_tensor(dst, src, hi_part.bitcast(fp32), ALU.subtract)

        def split_products(acc, a_hi, a_lo, b_hi, b_lo, first, last):
            nc.tensor.matmul(acc, a_hi, b_hi, start=first, stop=False)
            nc.tensor.matmul(acc, a_hi, b_lo, start=False, stop=False)
            return nc.tensor.matmul(acc, a_lo, b_hi, start=False, stop=last)

        w_loaded, b1_loaded = [sem(f"w_loaded{n}") for n in range(NV)], sem("b1_loaded")
        gp_setup = sem("gp_setup")
        wT_ready, wT_hi_done, wT_copied = sem("wT_ready"), sem("wT_hi_done"), sem("wT_copied")
        qkv_w_in, qkv_w_hi_done, qkv_w_split = sem("qkv_w_in"), sem("qkv_w_hi_done"), sem("qkv_w_split")
        const_done, wo_bias_in = sem("const_done"), sem("wo_bias_in")

        part1 = ExitStack()
        def sb1(name, shape, dt=fp32):
            return part1.enter_context(nc.sbuf_tensor(name, shape, dt))
        xin = [sb1(f"xin{k}", [P, NV, F]) for k in range(2)]
        xT_hi = [sb1(f"xT_hi{k}", [P, NO, KC, P], fp32r) for k in range(2)]
        xT_lo = [sb1(f"xT_lo{k}", [P, NO, KC, P], fp32r) for k in range(2)]
        square = [sb1(f"square{k}", [P, NV, F]) for k in range(2)]
        norms2 = [sb1(f"norms2{k}", [P, NV]) for k in range(2)]
        inv_norm = [sb1(f"inv_norm{k}", [P, NV]) for k in range(2)]
        simT_hi = [sb1(f"simT_hi{k}", [P, NO, P], fp32r) for k in range(2)]
        simT_lo = [sb1(f"simT_lo{k}", [P, NO, P], fp32r) for k in range(2)]
        proj_hi = [sb1(f"proj_hi{k}", [P, NO, E], fp32r) for k in range(2)]
        proj_lo = [sb1(f"proj_lo{k}", [P, NO, E], fp32r) for k in range(2)]
        base = [sb1(f"base{k}", [P, E]) for k in range(2)]
        h = [sb1(f"h{k}", [P, E]) for k in range(2)]
        bn = sb1("bn", [P, 6])
        mean_var = [sb1(f"mean_var{k}", [P, 2]) for k in range(2)]
        ln_scale = sb1("ln_scale", [P, 2])
        xn = [sb1(f"xn{k}", [P, E]) for k in range(2)]
        xnT_hi = [sb1(f"xnT_hi{k}", [P, KC, P], fp32r) for k in range(2)]
        xnT_lo = [sb1(f"xnT_lo{k}", [P, KC, P], fp32r) for k in range(2)]
        w_in = sb1("w_in", [P, E // P, NV * F])
        b1_in = sb1("b1_in", [NE * HC, P])

        x_loaded = [sem(f"x_loaded{k}") for k in range(2)]
        x01_ready, x01_hi_done, x01_lo_done = sem("x01_ready"), sem("x01_hi_done"), sem("x01_lo_done")
        x23_ready, x23_hi_done, x23_lo_done = sem("x23_ready"), sem("x23_hi_done"), sem("x23_lo_done")
        squares_done, clamped, inv_norm_ready = sem("squares_done"), sem("clamped"), sem("inv_norm_ready")
        dots_ready, base_ready = sem("dots_ready"), sem("base_ready")
        dots_hi_done, dots_lo_done, base_copied = sem("dots_hi_done"), sem("dots_lo_done"), sem("base_copied")
        mix_ready, h_ready = sem("mix_ready"), sem("h_ready")
        bn_done, stats_ready = sem("bn_done"), sem("stats_ready")
        rstd1_done, shift1_done, xn_ready, hb_done = sem("rstd1_done"), sem("shift1_done"), sem("xn_ready"), sem("hb_done")
        xnT_ready, xnT_hi_done, xnT_lo_done = sem("xnT_ready"), sem("xnT_hi_done"), sem("xnT_lo_done")
        qkv_ready, qkv_stored = sem("qkv_ready"), sem("qkv_stored")

        x01_ps, x23_ps = bank[0], bank[1]
        base_ps, mix_ps = bank[2], bank[3]
        xn_ps = wide[:, 3, :]
        LAG1 = 3

        with nc.Block() as block:
            @block.sync
            def _(sp):
                for n in range(NV):
                    cols = slice(n * F, (n + 1) * F)
                    sp.dma_start(w_in[:, :, cols], tok_W[:, cols].rearrange("(a p) n -> p a n", p=P)).then_inc(w_loaded[n], 16)
                sp.dma_start(b1_in[:, :], b1.rearrange("e (c p) -> (e c) p", p=P)).then_inc(b1_loaded, 16)

                def step(i, u):
                    if v := visit(i, u, 0, B):
                        b, use, k = v
                        wait(sp, x23_ready, b - 1)
                        wait(sp, squares_done, b - 1)
                        sp.dma_start(xin[k][:, :, :], x[b].rearrange("n s f -> s n f")).then_inc(x_loaded[k], 16)

                run_steps(sp, B, 0, step)

            @block.gpsimd
            def _(gp):
                gp.memset(ident[:, :], 0.0).then_inc(gp_setup, 1)
                gp.memset(identb[:, :], 0.0).then_inc(gp_setup, 1)
                gp.memset(ones[:, :], 1.0).then_inc(gp_setup, 1)
                gp.memset(minus_half[:, :], -0.5).then_inc(gp_setup, 1)
                gp.wait_ge(gp_setup, 4)
                for t in (ident, identb):
                    gp.affine_select(out=t[:, :], in_=t[:, :], compare_op=ALU.not_equal, fill=1.0,
                                     base=0, pattern=[[-1, P]], channel_multiplier=1).then_inc(gp_setup, 1)
                gp.affine_select(out=before[:, :], in_=ones[:, :], compare_op=ALU.is_gt, fill=0.0,
                                 base=0, pattern=[[1, P]], channel_multiplier=-1).then_inc(gp_setup, 1)
                gp.dma_start(wo_bias[:, :], bo.partition_broadcast(P)).then_inc(wo_bias_in, 16)
                gp.wait_ge(wo_bias_in, 16)

                def step(i, u):
                    if v := visit(i, u, 2, B):
                        b, use, k = v
                        wait(gp, stats_ready, b + 1)
                        wait_alone(gp, xn_ready, b)
                        gp.tensor_scalar_add(ln_scale[:, 0:1], mean_var[k][:, 1:2], EPS).then_inc(rstd1_done, 1)
                        wait_alone(gp, rstd1_done, 2 * b + 1)
                        gp.tensor_tensor(ln_scale[:, 0:1], ln_scale[:, 0:1], minus_half[:, 0:1],
                                         ALU.pow).then_inc(rstd1_done, 1)
                        wait_alone(gp, rstd1_done, 2 * b + 2)
                        gp.tensor_scalar(ln_scale[:, 1:2], mean_var[k][:, 0:1], ln_scale[:, 0:1], -1.0,
                                         ALU.mult, ALU.mult).then_inc(shift1_done, 1)
                        wait(gp, shift1_done, b + 1)
                        wait_alone(gp, xnT_ready, b - 1)
                        gp.tensor_scalar(xn[k][:, :], h[k][:, :], ln_scale[:, 0:1], ln_scale[:, 1:2],
                                         ALU.mult, ALU.add).then_inc(xn_ready, 1)
                        gp.tensor_tensor(hb_all[:, b, :], h[k][:, :], wo_bias[:, :], ALU.add).then_inc(hb_done, 1)
                    if v := visit(i, u, 0, B):
                        b, use, k = v
                        wait(gp, squares_done, b + 1)
                        wait(gp, dots_lo_done, NO * (b - 1))
                        wait_alone(gp, h_ready, b - 1)
                        gp.tensor_scalar_max(norms2[k][:, :], norms2[k][:, :], TINY).then_inc(clamped, 1)
                        wait_alone(gp, clamped, b + 1)
                        gp.tensor_tensor(inv_norm[k][:, :], norms2[k][:, :], minus_half[:, :],
                                         ALU.pow).then_inc(inv_norm_ready, 1)

                run_steps(gp, B, LAG1, step)

            @block.tensor
            def _(pe):
                pe.wait_ge(gp_setup, 7)
                for n in range(NV):
                    pe.wait_ge(w_loaded[n], 16)
                    if n >= 2:
                        pe.wait_ge(wT_copied, n - 1)
                    for c in range(KC):
                        for a in range(E // P):
                            last = nc.tensor.transpose(bank[n % 2][:, (c * 2 + a) * P:(c * 2 + a + 1) * P],
                                                       w_in[:, a, n * F + c * P:n * F + (c + 1) * P], ident[:, :])
                    last.then_inc(wT_ready, 1)
                pe.wait_ge(b1_loaded, 16)
                nc.tensor.transpose(bank[2][:, 0:NE * HC], b1_in[:, :],
                                    ident[0:NE * HC, 0:NE * HC]).then_inc(wT_ready, 1)
                pe.wait_ge(wT_copied, NV + 1)

                def step(i, u):
                    if v := visit(i, u, 0, B):
                        b, use, k = v
                        pe.wait_ge(x_loaded[k], 16 * use + 16)
                        for half, ps, ready, copied in ((0, x01_ps, x01_ready, x01_lo_done),
                                                        (1, x23_ps, x23_ready, x23_lo_done)):
                            wait(pe, copied, b)
                            for n in range(2):
                                for c in range(KC):
                                    last = nc.tensor.transpose(ps[:, (n * KC + c) * P:(n * KC + c + 1) * P],
                                                               xin[k][:, 2 * half + n, c * P:(c + 1) * P], ident[:, :])
                            last.then_inc(ready, 1)
                    if v := visit(i, u, 2, B):
                        b, use, k = v
                        wait(pe, dots_lo_done, NO * b + NO)
                        wait(pe, h_ready, b)
                        for n in range(NO):
                            last = split_products(mix_ps[:, 0:E], simT_hi[k][:, n, :], simT_lo[k][:, n, :],
                                                  proj_hi[k][:, n, :], proj_lo[k][:, n, :], n == 0, n == NO - 1)
                        last.then_inc(mix_ready, 1)
                    if v := visit(i, u, 3, B):
                        b, use, k = v
                        wait(pe, xn_ready, b + 1)
                        wait(pe, qkv_stored, b)
                        for c in range(KC):
                            last = nc.tensor.transpose(xn_ps[:, c * P:(c + 1) * P], xn[k][:, c * P:(c + 1) * P],
                                                       ident[:, :])
                        last.then_inc(xnT_ready, 1)
                    if v := visit(i, u, 1, B):
                        b, use, k = v
                        wait(pe, x01_lo_done, b + 1)
                        wait(pe, x23_lo_done, b + 1)
                        for n in range(NO):
                            wait(pe, dots_lo_done, NO * (b - 1) + n + 1)
                            blocks = slice(0, 2 * STRIDE[n] + 1, STRIDE[n])
                            for c in range(KC):
                                last = split_products(wide[:, n, 0:3 * P], xT_hi[k][:, n, c, :], xT_lo[k][:, n, c, :],
                                                      moving_hi[k][:, c, blocks, :], moving_lo[k][:, c, blocks, :],
                                                      c == 0, c == KC - 1)
                            last.then_inc(dots_ready, 1)
                        wait(pe, base_copied, b)
                        for c in range(KC):
                            last = split_products(base_ps[:, 0:E], moving_hi[k][:, c, 0, :], moving_lo[k][:, c, 0, :],
                                                  w0T_hi[:, c, :], w0T_lo[:, c, :], c == 0, c == KC - 1)
                        last.then_inc(base_ready, 1)
                    if v := visit(i, u, 3, B):
                        b, use, k = v
                        wait(pe, xnT_lo_done, b + 1)
                        if isinstance(b, int):
                            pe.wait_ge(qkv_w_split, 1)
                        for c in range(KC):
                            last = split_products(xn_ps[:, 0:QKV], xnT_hi[k][:, c, :], xnT_lo[k][:, c, :],
                                                  qkv_w_hi[:, c, :], qkv_w_lo[:, c, :], c == 0, c == KC - 1)
                        last.then_inc(qkv_ready, 1)

                run_steps(pe, B, LAG1, step)

            @block.scalar
            def _(act):
                chunks = "(c p) n -> p c n"
                for dst, src in ((qkv_w[:, :, 0:E], Wq), (qkv_w[:, :, E:E + DK], Wk), (qkv_w[:, :, E + DK:], Wv)):
                    act.dma_start(dst, src.rearrange(chunks, p=P)).then_inc(qkv_w_in, 16)
                for dst, src in ((tok_bias[:, :], tok_b), (qkv_bias[:, 0:E], bq), (qkv_bias[:, E:E + DK], bk),
                                 (qkv_bias[:, E + DK:], bv), (gate_bias[:, :], bg)):
                    act.dma_start(dst, src.partition_broadcast(P)).then_inc(const_done, 16)
                for dst, src in ((wo_w[:, :, :], Wo), (gate_w[:, :, :], Wg)):
                    act.dma_start(dst, src.rearrange(chunks, p=P)).then_inc(const_done, 16)
                for n in range(NV):
                    act.wait_ge(wT_ready, n + 1)
                    src = bank[n % 2][:, :].rearrange("p (c a s) -> p c a s", c=KC, a=E // P)
                    if n == 0:
                        last = nc.scalar.copy(w0T_hi[:, :, :].rearrange("p c (a s) -> p c a s", s=P), src)
                    else:
                        blocks = slice(STRIDE[n - 1], 2 * STRIDE[n - 1] + 1, STRIDE[n - 1])
                        for k in range(2):
                            last = nc.scalar.copy(moving_hi[k][:, :, blocks, :], src)
                    last.then_inc(wT_hi_done, 1)

                def step(i, u):
                    if v := visit(i, u, 0, B):
                        b, use, k = v
                        wait(act, x01_ready, b + 1)
                        wait(act, base_ready, b - 1)
                        nc.scalar.copy(moving_hi[k][:, :, 0, :],
                                       x01_ps[:, 0:KC * P].rearrange("p (c s) -> p c s", c=KC))
                        nc.scalar.copy(xT_hi[k][:, 0, :, :],
                                       x01_ps[:, KC * P:2 * KC * P].rearrange("p (c s) -> p c s", c=KC)).then_inc(x01_hi_done, 1)
                        wait(act, x23_ready, b + 1)
                        nc.scalar.copy(xT_hi[k][:, 1:3, :, :],
                                       x23_ps[:, :].rearrange("p (n c s) -> p n c s", n=2, c=KC)).then_inc(x23_hi_done, 1)
                    if v := visit(i, u, 3, B):
                        b, use, k = v
                        wait(act, xnT_ready, b + 1)
                        wait(act, qkv_ready, b - 1)
                        nc.scalar.copy(xnT_hi[k][:, :, :],
                                       xn_ps[:, 0:KC * P].rearrange("p (c s) -> p c s", c=KC)).then_inc(xnT_hi_done, 1)
                        if isinstance(b, int) and b == 0:
                            act.wait_ge(qkv_w_in, 48)
                            nc.scalar.copy(qkv_w_hi[:, :, :], qkv_w[:, :, :]).then_inc(qkv_w_hi_done, 1)
                    if v := visit(i, u, 0, B):
                        b, use, k = v
                        act.wait_ge(x_loaded[k], 16 * use + 16)
                        wait(act, inv_norm_ready, b - 1)
                        for n in range(NV):
                            last = nc.scalar.activation(square[k][:, n, :], xin[k][:, n, :], ACT.Square,
                                                        accum_out=norms2[k][:, n:n + 1])
                        last.then_inc(squares_done, 1)
                    if v := visit(i, u, 1, B):
                        b, use, k = v
                        wait(act, inv_norm_ready, b + 1)
                        wait(act, mix_ready, b - 1)
                        for n in range(NO):
                            wait(act, dots_ready, NO * b + n + 1)
                            nc.scalar.activation(simT_hi[k][:, n, :], wide[:, n, 0:P], ACT.Copy,
                                                 scale=inv_norm[k][:, n + 1:n + 2])
                            nc.scalar.copy(proj_hi[k][:, n, :], wide[:, n, P:3 * P]).then_inc(dots_hi_done, 1)

                run_steps(act, B, LAG1, step)

            @block.vector
            def _(dve):
                for n in range(NV):
                    dve.wait_ge(wT_hi_done, n + 1)
                    src = bank[n % 2][:, :].rearrange("p (c a s) -> p c a s", c=KC, a=E // P)
                    if n == 0:
                        by_block = "p c (a s) -> p c a s"
                        last = low_part(w0T_lo[:, :, :].rearrange(by_block, s=P), src, w0T_hi[:, :, :].rearrange(by_block, s=P))
                    else:
                        blocks = slice(STRIDE[n - 1], 2 * STRIDE[n - 1] + 1, STRIDE[n - 1])
                        for k in range(2):
                            last = low_part(moving_lo[k][:, :, blocks, :], src, moving_hi[k][:, :, blocks, :])
                    last.then_inc(wT_copied, 1)
                dve.wait_ge(wT_ready, NV + 1)
                nc.vector.tensor_copy(b1T[:, :], bank[2][:, 0:NE * HC]).then_inc(wT_copied, 1)

                def step(i, u):
                    if v := visit(i, u, 0, B):
                        b, use, k = v
                        wait(dve, x01_hi_done, b + 1)
                        wait(dve, base_ready, b - 1)
                        low_part(moving_lo[k][:, :, 0, :], x01_ps[:, 0:KC * P].rearrange("p (c s) -> p c s", c=KC),
                                 moving_hi[k][:, :, 0, :])
                        low_part(xT_lo[k][:, 0, :, :], x01_ps[:, KC * P:2 * KC * P].rearrange("p (c s) -> p c s", c=KC),
                                 xT_hi[k][:, 0, :, :]).then_inc(x01_lo_done, 1)
                        wait(dve, x23_hi_done, b + 1)
                        low_part(xT_lo[k][:, 1:3, :, :], x23_ps[:, :].rearrange("p (n c s) -> p n c s", n=2, c=KC),
                                 xT_hi[k][:, 1:3, :, :]).then_inc(x23_lo_done, 1)
                    if v := visit(i, u, 2, B):
                        b, use, k = v
                        wait(dve, mix_ready, b + 1)
                        wait(dve, base_copied, b + 1)
                        wait(dve, xn_ready, b - 1)
                        wait(dve, hb_done, b - 1)
                        nc.vector.scalar_tensor_tensor(out=h[k][:, :], in0=mix_ps[:, 0:E], scalar=inv_norm[k][:, 0:1],
                                                       in1=base[k][:, :], op0=ALU.mult, op1=ALU.add).then_inc(h_ready, 1)
                        wait(dve, h_ready, b + 1)
                        nc.vector.bn_stats(bn[:, :], h[k][:, :]).then_inc(bn_done, 1)
                        wait_alone(dve, bn_done, b + 1)
                        nc.vector.bn_aggr(mean_var[k][:, :], bn[:, :]).then_inc(stats_ready, 1)
                    if v := visit(i, u, 3, B):
                        b, use, k = v
                        wait(dve, xnT_hi_done, b + 1)
                        wait(dve, qkv_ready, b - 1)
                        low_part(xnT_lo[k][:, :, :], xn_ps[:, 0:KC * P].rearrange("p (c s) -> p c s", c=KC),
                                 xnT_hi[k][:, :, :]).then_inc(xnT_lo_done, 1)
                        if isinstance(b, int) and b == 0:
                            dve.wait_ge(qkv_w_hi_done, 1)
                            low_part(qkv_w_lo[:, :, :], qkv_w[:, :, :], qkv_w_hi[:, :, :]).then_inc(qkv_w_split, 1)
                            dve.wait_ge(const_done, 16 * 7)
                    if v := visit(i, u, 1, B):
                        b, use, k = v
                        wait(dve, mix_ready, b - 1)
                        for n in range(NO):
                            wait(dve, dots_hi_done, NO * b + n + 1)
                            nc.vector.scalar_tensor_tensor(out=simT_lo[k][:, n, :], in0=wide[:, n, 0:P],
                                                           scalar=inv_norm[k][:, n + 1:n + 2],
                                                           in1=simT_hi[k][:, n, :].bitcast(fp32),
                                                           op0=ALU.mult, op1=ALU.subtract)
                            low_part(proj_lo[k][:, n, :], wide[:, n, P:3 * P], proj_hi[k][:, n, :]).then_inc(dots_lo_done, 1)
                        wait(dve, base_ready, b + 1)
                        if isinstance(b, int):
                            dve.wait_ge(const_done, 16 * 7)
                        nc.vector.tensor_tensor(base[k][:, :], base_ps[:, 0:E], tok_bias[:, :],
                                                ALU.add).then_inc(base_copied, 1)
                    if v := visit(i, u, 3, B):
                        b, use, k = v
                        wait(dve, qkv_ready, b + 1)
                        nc.vector.tensor_tensor(qkv_all[:, b, :], xn_ps[:, 0:QKV], qkv_bias[:, :],
                                                ALU.add).then_inc(qkv_stored, 1)

                run_steps(dve, B, LAG1, step)
        part1.close()

        part2 = ExitStack()
        def sb2(name, shape, dt=fp32):
            return [part2.enter_context(nc.sbuf_tensor(f"{name}{k}", shape, dt)) for k in range(2)]
        q_parts = sb2("q_parts", [P, HEADS, TERMS, DK], bf16)
        k_parts = sb2("k_parts", [P, TERMS, DK], bf16)
        q_rest = sb2("q_rest", [P, HEADS, DK])
        k_rest = sb2("k_rest", [P, DK])
        v_one = sb2("v_one", [P, 32])
        qT = sb2("qT", [SROWS + MPARTS, HEADS, P], bf16)
        kT = sb2("kT", [SROWS + MPARTS, P], bf16)
        neg_max = sb2("neg_max", [P, HEADS])
        max_parts = sb2("max_parts", [P, MPARTS, HEADS], bf16)
        max_T = sb2("max_T", [MPARTS * HEADS, P], bf16)
        probs = sb2("probs", [P, HEADS, P])
        pvT = sb2("pvT", [P, HB, P])
        inv_sum = sb2("inv_sum", [P, HEADS])
        context = sb2("context", [P, HEADS, DK])
        contextT = sb2("contextT", [P, KC, P])
        row = sb2("row", [P, 2, E])
        bn2 = sb2("bn2_", [P, 6])
        mv2 = sb2("mv2_", [P, 2])
        ln2 = sb2("ln2_", [P, 2])
        xn2T = sb2("xn2T", [P, KC, P])

        q1_ready, q_rest_ready, q2_ready = sem("q1_ready"), sem("q_rest_ready"), sem("q2_ready")
        q_ready, k_chain, k_ready, v_ready = sem("q_ready"), sem("k_chain"), sem("k_ready"), sem("v_ready")
        qT_ready, kT_ready, kT_copied = sem("qT_ready"), sem("kT_ready"), sem("kT_copied")
        qT_copied = [sem(f"qT_copied{half}") for half in range(2)]
        s_ready, max_done, max_parts_ready = sem("s_ready"), sem("max_done"), sem("max_parts_ready")
        max1_done = sem("max1_done")
        maxT_ready, maxT_copied = sem("maxT_ready"), sem("maxT_copied")
        max_rows = [sem(f"max_rows{k}") for k in range(2)]
        sT_ready, exp_done, pv_ready, pvT_copied, pv_back, inv_sum_ready, context_ready = (
            sem("sT_ready"), sem("exp_done"), sem("pv_ready"), sem("pvT_copied"), sem("pv_back"), sem("inv_sum_ready"), sem("context_ready"))
        ctxT_ready, ctxT_copied, attn_ready, h2_ready = sem("ctxT_ready"), sem("ctxT_copied"), sem("attn_ready"), sem("h2_ready")
        bn2_done, stats2_ready, ln2_chain, xn2_ready = sem("bn2_done"), sem("stats2_ready"), sem("ln2_chain"), sem("xn2_ready")
        row_stored = [sem(f"row_stored{k}") for k in range(2)]
        xn2T_ready, xn2T_copied, gate_ready, gate_stored = sem("xn2T_ready"), sem("xn2T_copied"), sem("gate_ready"), sem("gate_stored")
        part2_const = sem("part2_const")

        q_ps = [bank[0][:, :].bitcast(bf16).rearrange("p (h s) -> p h s", s=P),
                bank[3][:, :].bitcast(bf16).rearrange("p (h s) -> p h s", s=P)]
        HH = HEADS // 2
        attn_ps, small_ps = bank[1], bank[2]
        small_bf = small_ps[:, :].bitcast(bf16)
        LAG2 = 5

        with nc.Block() as block:
            @block.sync
            def _(sp):
                def step(i, u):
                    if v := visit(i, u, 2, B):
                        b, use, k = v
                        wait(sp, maxT_copied, b + 1)
                        wait(sp, sT_ready, 2 * (b - 1))
                        for m in range(MPARTS):
                            sp.dma_start(qT[k][SROWS + m:SROWS + m + 1, :, :],
                                         max_T[k][m * HEADS:(m + 1) * HEADS, :]).then_inc(max_rows[k], 16)
                    if v := visit(i, u, 4, B):
                        b, use, k = v
                        wait(sp, h2_ready, b + 1)
                        sp.dma_start(residual_rows[bass.ds(b * P, P), :], row[k][:, 1, :]).then_inc(row_stored[k], 16)
                        wait(sp, xn2_ready, b + 1)
                        sp.dma_start(normed_rows[bass.ds(b * P, P), :], row[k][:, 0, :]).then_inc(row_stored[k], 16)

                run_steps(sp, B, LAG2, step)

            @block.gpsimd
            def _(gp):
                for k in range(2):
                    gp.memset(kT[k][SROWS:SROWS + MPARTS, :], 1.0).then_inc(part2_const, 1)
                    gp.wait_ge(part2_const, 3 * k + 1)
                    gp.memset(v_one[k][:, :], 0.0).then_inc(part2_const, 1)
                    gp.wait_ge(part2_const, 3 * k + 2)
                    gp.memset(v_one[k][:, DK:DK + 1], 1.0).then_inc(part2_const, 1)
                    gp.wait_ge(part2_const, 3 * k + 3)

                def step(i, u):
                    if v := visit(i, u, 0, B):
                        b, use, k = v
                        qb = qkv_all[:, b, 0:E].rearrange("p (h d) -> p h d", d=DK)
                        wait(gp, q1_ready, b + 1)
                        wait_alone(gp, q_ready, b - 1)
                        gp.tensor_tensor(q_rest[k][:, :, :], qb, q_parts[k][:, :, 0, :], ALU.subtract).then_inc(q_rest_ready, 1)
                        wait_alone(gp, q2_ready, b + 1)
                        gp.tensor_tensor(q_parts[k][:, :, 5, :], q_rest[k][:, :, :], q_parts[k][:, :, 3, :],
                                         ALU.subtract).then_inc(q_ready, 1)
                    if v := visit(i, u, 0, B):
                        b, use, k = v
                        kb = qkv_all[:, b, E:E + DK]
                        k3 = lambda a, n: a.unsqueeze(1).broadcast_to([P, n, DK])
                        wait(gp, kT_ready, b - 1)
                        wait_alone(gp, k_ready, b - 1)
                        gp.tensor_copy(k_parts[k][:, 1:TERMS:2, :], k3(kb, 3)).then_inc(k_chain, 1)
                        wait_alone(gp, k_chain, 3 * b + 1)
                        gp.tensor_tensor(k_rest[k][:, :], kb, k_parts[k][:, 1, :], ALU.subtract).then_inc(k_chain, 1)
                        wait_alone(gp, k_chain, 3 * b + 2)
                        gp.tensor_copy(k_parts[k][:, 2:TERMS:2, :], k3(k_rest[k][:, :], 2)).then_inc(k_chain, 1)
                        wait_alone(gp, k_chain, 3 * b + 3)
                        gp.tensor_tensor(k_parts[k][:, 0, :], k_rest[k][:, :], k_parts[k][:, 2, :],
                                         ALU.subtract).then_inc(k_ready, 1)
                    if v := visit(i, u, 4, B):
                        b, use, k = v
                        wait_alone(gp, stats2_ready, b + 1)
                        gp.tensor_scalar_add(ln2[k][:, 0:1], mv2[k][:, 1:2], EPS).then_inc(ln2_chain, 1)
                        wait_alone(gp, ln2_chain, 3 * b + 1)
                        gp.tensor_tensor(ln2[k][:, 0:1], ln2[k][:, 0:1], minus_half[:, 0:1],
                                         ALU.pow).then_inc(ln2_chain, 1)
                        wait_alone(gp, ln2_chain, 3 * b + 2)
                        gp.tensor_scalar(ln2[k][:, 1:2], mv2[k][:, 0:1], ln2[k][:, 0:1], -1.0,
                                         ALU.mult, ALU.mult).then_inc(ln2_chain, 1)
                        wait_alone(gp, ln2_chain, 3 * b + 3)
                        gp.tensor_scalar(row[k][:, 0, :], row[k][:, 1, :], ln2[k][:, 0:1], ln2[k][:, 1:2],
                                         ALU.mult, ALU.add).then_inc(xn2_ready, 1)
                    if v := visit(i, u, 2, B):
                        b, use, k = v
                        wait_alone(gp, pv_ready, b - 1)
                        gp.tensor_copy(v_one[k][:, 0:DK], qkv_all[:, b, E + DK:]).then_inc(v_ready, 1)

                run_steps(gp, B, LAG2, step)
                for k in range(2):
                    gp.wait_ge(row_stored[k], 32 * (B // 2))

            @block.tensor
            def _(pe):
                pe.wait_ge(part2_const, 6)

                def q_transposes(half, b, k):
                    wait(pe, q_ready, b + 1)
                    wait(pe, qT_copied[half], b)
                    for n in range(HH):
                        last = nc.tensor.transpose(q_ps[half][0:SROWS, n, :],
                                                   q_parts[k][:, half * HH + n, :, :].rearrange("p t d -> p (t d)"), identb[:, :])
                    last.then_inc(qT_ready, 1)

                def step(i, u):
                    if v := visit(i, u, 1, B):
                        b, use, k = v
                        q_transposes(0, b, k)
                    if v := visit(i, u, 4, B):
                        b, use, k = v
                        wait(pe, pvT_copied, b + 1)
                        for n in range(HB):
                            last = nc.tensor.transpose(attn_ps[:, n * P:(n + 1) * P], pvT[k][:, n, :], ident[:, :])
                        last.then_inc(pv_back, 1)
                    if v := visit(i, u, 3, B):
                        b, use, k = v
                        pe.wait_ge(max_rows[k], 16 * MPARTS * (use + 1))
                        for n in range(4):
                            wait(pe, max_done, at_most(2 * (b + 1) + n // 2 + 1, 2 * B))
                            wait(pe, exp_done, 2 * (b - 1) + n // 2 + 1)
                            last = nc.tensor.matmul(wide[:, n, :], kT[k][:, :],
                                                    qT[k][:, n * HB:(n + 1) * HB, :].rearrange("r h s -> r (h s)"),
                                                    start=True, stop=True)
                            if n % 2:
                                last.then_inc(sT_ready, 1)
                    if v := visit(i, u, 1, B):
                        b, use, k = v
                        q_transposes(1, b, k)
                    if v := visit(i, u, 1, B):
                        b, use, k = v
                        wait(pe, k_ready, b + 1)
                        wait(pe, gate_stored, b - 4)
                        wait(pe, maxT_copied, b - 1)
                        nc.tensor.transpose(small_bf[0:SROWS, 0:P], k_parts[k][:, :, :].rearrange("p t d -> p (t d)"),
                                            identb[:, :]).then_inc(kT_ready, 1)
                    if v := visit(i, u, 4, B):
                        b, use, k = v
                        wait(pe, context_ready, b + 1)
                        for c in range(KC):
                            last = nc.tensor.transpose(attn_ps[:, c * P:(c + 1) * P],
                                                       context[k][:, :, :].rearrange("p h d -> p (h d)")[:, c * P:(c + 1) * P],
                                                       ident[:, :])
                        last.then_inc(ctxT_ready, 1)
                    if v := visit(i, u, 2, B):
                        b, use, k = v
                        wait(pe, max_parts_ready, b + 1)
                        wait(pe, kT_copied, at_most(b + 2, B))
                        wait(pe, gate_stored, b - 3)
                        nc.tensor.transpose(small_bf[0:MPARTS * HEADS, 0:P],
                                            max_parts[k][:, :, :].rearrange("p m h -> p (m h)"),
                                            identb[:, :]).then_inc(maxT_ready, 1)
                    if v := visit(i, u, 4, B):
                        b, use, k = v
                        wait(pe, ctxT_copied, b + 1)
                        for c in range(KC):
                            last = nc.tensor.matmul(attn_ps[:, 0:E], contextT[k][:, c, :], wo_w[:, c, :],
                                                    start=(c == 0), stop=(c == KC - 1))
                        last.then_inc(attn_ready, 1)
                    if v := visit(i, u, 5, B):
                        b, use, k = v
                        wait(pe, xn2_ready, b + 1)
                        wait(pe, maxT_copied, at_most(b + 4, B))
                        wait(pe, kT_copied, at_most(b + 5, B))
                        wait(pe, gate_stored, b)
                        for c in range(KC):
                            last = nc.tensor.transpose(small_ps[:, c * P:(c + 1) * P], row[k][:, 0, c * P:(c + 1) * P],
                                                       ident[:, :])
                        last.then_inc(xn2T_ready, 1)
                    if v := visit(i, u, 1, B):
                        b, use, k = v
                        wait(pe, qT_copied[0], b + 1)
                        wait(pe, qT_copied[1], b + 1)
                        wait(pe, kT_copied, b + 1)
                        for n in range(4):
                            wait(pe, exp_done, 2 * (b - 2) + n // 2 + 1)
                            for hh in range(HB):
                                last = nc.tensor.matmul(wide[:, n, hh * P:(hh + 1) * P], qT[k][0:SROWS, n * HB + hh, :],
                                                        kT[k][0:SROWS, :], start=True, stop=True)
                            if n % 2:
                                last.then_inc(s_ready, 1)
                    if v := visit(i, u, 3, B):
                        b, use, k = v
                        wait(pe, exp_done, 2 * b + 2)
                        wait(pe, v_ready, b + 1)
                        wait(pe, h2_ready, b)
                        for n in range(4):
                            last = nc.tensor.matmul(attn_ps[32 * n:32 * (n + 1), :], v_one[k][:, :],
                                                    probs[k][:, n * HB:(n + 1) * HB, :].rearrange("p h s -> p (h s)"),
                                                    start=True, stop=True)
                        last.then_inc(pv_ready, 1)
                    if v := visit(i, u, 5, B):
                        b, use, k = v
                        wait(pe, xn2T_copied, b + 1)
                        for c in range(KC):
                            last = nc.tensor.matmul(small_ps[:, 0:NE], xn2T[k][:, c, :], gate_w[:, c, :],
                                                    start=(c == 0), stop=(c == KC - 1))
                        last.then_inc(gate_ready, 1)

                run_steps(pe, B, LAG2, step)

            @block.scalar
            def _(act):
                nc.scalar.preload_act_table(ACT.Exp)

                def exp_half(n, b, k):
                    wait(act, sT_ready, 2 * b + n + 1)
                    wait(act, pv_ready, b - 1)
                    nc.scalar.activation(probs[k][:, n * HH:(n + 1) * HH, :],
                                         wide[:, 2 * n:2 * n + 2, :].rearrange("p a (h s) -> p (a h) s", s=P),
                                         ACT.Exp, scale=SCALE).then_inc(exp_done, 1)

                def step(i, u):
                    if v := visit(i, u, 0, B):
                        b, use, k = v
                        wait(act, qT_ready, 2 * (b - 1))
                        nc.scalar.copy(q_parts[k][:, :, 0:3, :],
                                       qkv_all[:, b, 0:E].rearrange("p (h d) -> p h d", d=DK)
                                       .unsqueeze(2).broadcast_to([P, HEADS, 3, DK])).then_inc(q1_ready, 1)
                    if v := visit(i, u, 3, B):
                        b, use, k = v
                        exp_half(0, b, k)
                    if v := visit(i, u, 4, B):
                        b, use, k = v
                        wait(act, ctxT_ready, b + 1)
                        wait(act, attn_ready, b - 1)
                        nc.scalar.copy(contextT[k][:, :, :],
                                       attn_ps[:, 0:KC * P].rearrange("p (c s) -> p c s", c=KC)).then_inc(ctxT_copied, 1)
                    if v := visit(i, u, 1, B):
                        b, use, k = v
                        wait(act, qT_ready, 2 * b + 2)
                        wait(act, sT_ready, 2 * (b - 1))
                        nc.scalar.copy(qT[k][0:SROWS, HH:HEADS, :], q_ps[1][0:SROWS, :, :]).then_inc(qT_copied[1], 1)
                    if v := visit(i, u, 2, B):
                        b, use, k = v
                        wait(act, maxT_ready, b + 1)
                        if not isinstance(use, int) or use > 0:
                            act.wait_ge(max_rows[k], 16 * MPARTS * use)
                        nc.scalar.copy(max_T[k][:, :], small_bf[0:MPARTS * HEADS, 0:P]).then_inc(maxT_copied, 1)
                    if v := visit(i, u, 3, B):
                        b, use, k = v
                        exp_half(1, b, k)
                    if v := visit(i, u, 0, B):
                        b, use, k = v
                        wait(act, q_rest_ready, b + 1)
                        nc.scalar.copy(q_parts[k][:, :, 3:5, :],
                                       q_rest[k][:, :, :].unsqueeze(2).broadcast_to([P, HEADS, 2, DK])).then_inc(q2_ready, 1)
                    if v := visit(i, u, 5, B):
                        b, use, k = v
                        wait(act, xn2T_ready, b + 1)
                        wait(act, gate_ready, b - 1)
                        nc.scalar.copy(xn2T[k][:, :, :],
                                       small_ps[:, 0:KC * P].rearrange("p (c s) -> p c s", c=KC)).then_inc(xn2T_copied, 1)
                    if v := visit(i, u, 3, B):
                        b, use, k = v
                        wait(act, pv_ready, b + 1)
                        wait(act, pv_back, b - 1)
                        nc.scalar.copy(pvT[k][:, :, :], attn_ps[:, :].rearrange("p (h s) -> p h s", s=P)).then_inc(pvT_copied, 1)

                run_steps(act, B, LAG2, step)

            @block.vector
            def _(dve):
                def step(i, u):
                    if v := visit(i, u, 4, B):
                        b, use, k = v
                        pv = attn_ps[:, :].rearrange("p (n j d) -> p j n d", n=HB, j=4)
                        wait(dve, pv_back, b + 1)
                        wait(dve, ctxT_ready, b - 1)
                        nc.vector.reciprocal(inv_sum[k][:, :].rearrange("p (j n) -> p j n", j=4),
                                             pv[:, :, :, DK]).then_inc(inv_sum_ready, 1)
                        wait(dve, inv_sum_ready, b + 1)
                        nc.vector.tensor_tensor(context[k][:, :, :].rearrange("p (j n) d -> p j n d", j=4), pv[:, :, :, 0:DK],
                                                inv_sum[k][:, :].rearrange("p (j n) -> p j n", j=4)
                                                .unsqueeze(3).broadcast_to([P, 4, HB, DK]),
                                                ALU.mult).then_inc(context_ready, 1)
                    if v := visit(i, u, 1, B):
                        b, use, k = v
                        wait(dve, kT_ready, b + 1)
                        wait(dve, sT_ready, 2 * (b - 1))
                        nc.vector.tensor_copy(kT[k][0:SROWS, :], small_bf[0:SROWS, 0:P]).then_inc(kT_copied, 1)
                    if v := visit(i, u, 1, B):
                        b, use, k = v
                        wait(dve, qT_ready, 2 * b + 1)
                        wait(dve, sT_ready, 2 * (b - 1))
                        nc.vector.tensor_copy(qT[k][0:SROWS, 0:HH, :], q_ps[0][0:SROWS, :, :]).then_inc(qT_copied[0], 1)
                    if v := visit(i, u, 4, B):
                        b, use, k = v
                        wait(dve, attn_ready, b + 1)
                        if not isinstance(use, int) or use > 0:
                            dve.wait_ge(row_stored[k], 32 * use)
                        wait(dve, xn2T_ready, b - 1)
                        nc.vector.tensor_tensor(row[k][:, 1, :], attn_ps[:, 0:E], hb_all[:, b, :],
                                                ALU.add).then_inc(h2_ready, 1)
                        wait(dve, h2_ready, b + 1)
                        nc.vector.bn_stats(bn2[k][:, :], row[k][:, 1, :]).then_inc(bn2_done, 1)
                        wait(dve, bn2_done, b + 1)
                        wait_alone(dve, xn2_ready, b - 1)
                        nc.vector.bn_aggr(mv2[k][:, :], bn2[k][:, :]).then_inc(stats2_ready, 1)
                    if v := visit(i, u, 1, B):
                        b, use, k = v
                        for n in range(2):
                            wait(dve, s_ready, 2 * b + n + 1)
                            wait(dve, max_parts_ready, b - 1)
                            nc.vector.tensor_reduce(out=neg_max[k][:, n * HH:(n + 1) * HH],
                                                    in_=wide[:, 2 * n:2 * n + 2, :].rearrange("p a (h s) -> p (a h) s", s=P),
                                                    axis=AX.X, op=ALU.max, negate=True).then_inc(max_done, 1)
                        wait(dve, max_done, 2 * b + 2)
                        wait(dve, maxT_ready, b - 1)
                        nc.vector.tensor_copy(max_parts[k][:, 0, :], neg_max[k][:, :]).then_inc(max1_done, 1)
                        wait(dve, max1_done, b + 1)
                        nc.vector.tensor_tensor(max_parts[k][:, 1, :], neg_max[k][:, :], max_parts[k][:, 0, :],
                                                ALU.subtract).then_inc(max_parts_ready, 1)
                    if v := visit(i, u, 5, B):
                        b, use, k = v
                        wait(dve, gate_ready, b + 1)
                        nc.vector.tensor_tensor(logits[:, b, :], small_ps[:, 0:NE], gate_bias[:, :],
                                                ALU.add).then_inc(gate_stored, 1)

                run_steps(dve, B, LAG2, step)
        part2.close()

        front.close()
        w1_in = pair("w1_in", [P, KC, HID])
        w1_hi, w1_lo = pair("w1_hi", [P, KC, HID], fp32r), pair("w1_lo", [P, KC, HID], fp32r)
        w2_in = pair("w2_in", [P, HC, E])
        w2_hi, w2_lo = pair("w2_hi", [P, HC, E], fp32r), pair("w2_lo", [P, HC, E], fp32r)
        b2_rows = pair("b2_rows", [P, E])
        b1_cols = pair("b1_cols", [P, HC])
        gather_ids = [pair(f"gather_ids{m}_", [P, 1], i32) for m in range(SUBS)]
        scatter_ids = [pair(f"scatter_ids{m}_", [P, 1], i32) for m in range(SUBS)]
        weights = pair("weights", [P, SUBS])
        normed = [pair(f"normed{m}_", [P, E]) for m in range(SUBS)]
        residual = [pair(f"residual{m}_", [P, E]) for m in range(SUBS)]
        slotT_hi, slotT_lo = pair("slotT_hi", [P, KC, SLOT_TOKENS], fp32r), pair("slotT_lo", [P, KC, SLOT_TOKENS], fp32r)
        hidden = sb("hidden", [P, HC, SLOT_TOKENS])
        hidden_hi, hidden_lo = pair("hidden_hi", [P, HC, SLOT_TOKENS], fp32r), pair("hidden_lo", [P, HC, SLOT_TOKENS], fp32r)
        plus_b2 = [pair(f"plus_b2_{m}_", [P, E]) for m in range(SUBS)]
        finished = [pair(f"finished{m}_", [P, E]) for m in range(SUBS)]

        w1_loaded = [sem(f"w1_loaded{k}") for k in range(2)]
        w2_loaded = [sem(f"w2_loaded{k}") for k in range(2)]
        b2_loaded = [sem(f"b2_loaded{k}") for k in range(2)]
        normed_in = [[sem(f"normed_in{m}_{k}") for k in range(2)] for m in range(SUBS)]
        residual_in = [[sem(f"residual_in{m}_{k}") for k in range(2)] for m in range(SUBS)]
        scattered = [[sem(f"scattered{m}_{k}") for k in range(2)] for m in range(SUBS)]
        w1_hi_ready, w1_lo_ready = sem("w1_hi_ready"), sem("w1_lo_ready")
        w2_hi_ready, w2_lo_ready = sem("w2_hi_ready"), sem("w2_lo_ready")
        rows_cleared, gather_ids_ready, scatter_ids_ready = sem("rows_cleared"), sem("gather_ids_ready"), sem("scatter_ids_ready")
        slotT_ready, slotT_hi_ready, slotT_lo_ready = sem("slotT_ready"), sem("slotT_hi_ready"), sem("slotT_lo_ready")
        picks_ready, up_ready, down_ready = sem("picks_ready"), sem("up_ready"), sem("down_ready")
        silu_done, hidden_hi_ready, hidden_lo_ready = sem("silu_done"), sem("hidden_hi_ready"), sem("hidden_lo_ready")
        plus_b2_ready, finished_ready = sem("plus_b2_ready"), sem("finished_ready")
        slot_ps, down_ps = bank[0], [bank[1], bank[2]]
        PAIRS = HC // 2
        W2_PARTS = 2
        W2_C = HC // W2_PARTS
        W1_N = HID * KC // PAIRS
        LAG3 = 2


        token1 = sb("token1", [P, B])
        expert_rank = sb("expert_rank", [P, NE])
        slot_fill = sb("slot_fill", [P, FULL_SLOTS])
        block_no = sb("block_no", [P, BLOCKS])
        lane_no = sb("lane_no", [P, P])
        slot_no = sb("slot_no", [P, SLOTS])
        best = sb("best", [P, B])
        below = sb("below", [P, B, NE])
        expd = sb("expd", [P, B, NE])
        total = sb("total", [P, B])
        weight = sb("weight", [P, B])
        is_best = sb("is_best", [P, B, NE])
        chosen = sb("chosen", [P, B])
        onehot = sb("onehot", [P, B, NE], bf16)
        counts = sb("counts", [P, NE, B])
        running = sb("running", [P, NE, B])
        earlier = sb("earlier", [P, NE, B])
        n_tokens = sb("n_tokens", [P, NE])
        more_than = sb("more_than", [P, NE, FULL_SLOTS])
        n_slots = sb("n_slots", [P, NE])
        slot_end = sb("slot_end", [P, NE])
        first_row = sb("first_row", [P, NE])
        place = sb("place", [P, B, NE])
        picked = sb("picked", [P, B, NE])
        position = sb("position", [P, B])
        position_i = sb("position_i", [P, B], i32)
        block_i = sb("block_i", [P, B], i32)
        lane_i = sb("lane_i", [P, B], i32)
        block_f = sb("block_f", [P, B])
        lane_f = sb("lane_f", [P, B])
        weight_hi, weight_lo = sb("weight_hi", [P, B], fp32r), sb("weight_lo", [P, B], fp32r)
        in_lane = [hidden_hi[k][:, :, :].rearrange("p c s -> p (c s)").rearrange("p (b l) -> p b l", l=P) for k in range(2)]
        VALUES = 3
        in_block = sb("in_block", [P, B, VALUES, BLOCKS], fp32r)
        at_block = sb("at_block", [P, B, BLOCKS])
        weight_sum = sb("weight_sum", [P, BLOCKS])
        padding = sb("padding", [P, BLOCKS])
        row_id_f = sb("row_id_f", [P, BLOCKS])
        past = sb("past", [1, SLOTS, NE])
        slot_expert_f = sb("slot_expert_f", [1, SLOTS])

        iotas, r_chain, exp_ready = sem("iotas"), sem("r_chain"), sem("exp_ready")
        slot_expert_ready, row_table_ready = sem("slot_expert_ready"), sem("row_table_ready")
        below_ready, onehot_ready, ranks_ready = sem("below_ready"), sem("onehot_ready"), sem("ranks_ready")
        lanes_ready, table_ready = sem("lanes_ready"), sem("table_ready")
        at_block_ready, weights_ready = sem("at_block_ready"), sem("weights_ready")
        rank_ps, count_ps, table_ps = bank[0], bank[1], bank[2]
        GROUPS = 4
        GB = B // GROUPS

        with nc.Block() as block:
            @block.sync
            def _(sp):
                sp.wait_ge(slot_expert_ready, 1)

                def step(i, u):
                    if v := visit(i, u, 0, SLOTS):
                        s, use, k = v
                        e = sp.value_load(slot_expert[0:1, bass.ds(s, 1)], min_val=0, max_val=NE - 1)
                        wait(sp, w1_lo_ready, PAIRS * (s - 1))
                        sp.dma_start(w1_in[k][:, :, :], W1[e].rearrange("(c p) n -> p c n", p=P)).then_inc(w1_loaded[k], 16)
                        wait(sp, w2_lo_ready, W2_PARTS * (s - 1))
                        sp.dma_start(w2_in[k][:, :, :], W2[e].rearrange("(c p) n -> p c n", p=P)).then_inc(w2_loaded[k], 16)
                    if v := visit(i, u, 1, SLOTS):
                        s, use, k = v
                        e = sp.value_load(slot_expert[0:1, bass.ds(s, 1)], min_val=0, max_val=NE - 1)
                        wait(sp, plus_b2_ready, SUBS * (s - 1))
                        sp.dma_start(b2_rows[k][:, :], b2[e].partition_broadcast(P)).then_inc(b2_loaded[k], 16)

                run_steps(sp, SLOTS, 1, step)

            @block.gpsimd
            def _(gp):
                for dst, pattern, base in ((expert_rank[:, :], [[-1, NE]], NE),
                                           (slot_fill[:, :], [[SLOT_TOKENS, FULL_SLOTS]], 0),
                                           (block_no[:, :], [[1, BLOCKS]], 0), (lane_no[:, :], [[1, P]], 0),
                                           (slot_no[:, :], [[1, SLOTS]], 0)):
                    gp.iota(dst, pattern=pattern, base=base, channel_multiplier=0,
                            allow_small_or_imprecise_dtypes=True).then_inc(iotas, 1)
                gp.iota(token1[:, :], pattern=[[P, B]], base=1, channel_multiplier=1,
                        allow_small_or_imprecise_dtypes=True).then_inc(iotas, 1)
                for k in range(2):
                    for m in range(SUBS):
                        gp.memset(normed[m][k][:, :], 0.0).then_inc(rows_cleared, 1)
                        gp.memset(residual[m][k][:, :], 0.0).then_inc(rows_cleared, 1)
                gp.wait_ge(rows_cleared, 2 * 2 * SUBS)
                for g in range(GROUPS):
                    s = slice(g * GB, (g + 1) * GB)
                    gp.wait_ge(at_block_ready, g + 1)
                    for n, value in ((1, weight_hi), (2, weight_lo)):
                        last = gp.tensor_tensor(in_block[:, s, n, :], at_block[:, s, :],
                                                value[:, s].bitcast(fp32).unsqueeze(2).broadcast_to([P, GB, BLOCKS]), ALU.mult)
                    last.then_inc(weights_ready, 1)
                gp.wait_ge(row_table_ready, 1)

                def gather(dst, table, ids_):
                    return gp.indirect_dma_start(out=dst, out_offset=None, in_=table,
                                                 in_offset=bass.IndirectOffsetOnAxis(ap=ids_[:, 0:1], axis=0),
                                                 bounds_check=TOKENS - 1, oob_is_err=False)

                def step(i, u):
                    if v := visit(i, u, 0, SLOTS):
                        s, use, k = v
                        wait_alone(gp, slotT_ready, s - 1)
                        for m in range(SUBS):
                            if not isinstance(use, int) or use > 0:
                                wait_alone(gp, residual_in[m][k], 16 * use)
                            gp.tensor_copy(gather_ids[m][k][:, :], row_id[:, bass.ds(SUBS * s + m, 1)]).then_inc(gather_ids_ready, 1)
                            wait_alone(gp, gather_ids_ready, SUBS * s + m + 1)
                            gather(normed[m][k][:, :], normed_rows, gather_ids[m][k]).then_inc(normed_in[m][k], 16)
                    for m in range(SUBS):
                        if v := visit(i, u, 2, SLOTS):
                            s, use, k = v
                            if not isinstance(use, int) or use > 0:
                                wait_alone(gp, scattered[m][k], 16 * use)
                            gp.tensor_copy(scatter_ids[m][k][:, :], row_id[:, bass.ds(SUBS * s + m, 1)]).then_inc(scatter_ids_ready, 1)
                            wait_alone(gp, finished_ready, SUBS * s + m + 1)
                            wait_alone(gp, scatter_ids_ready, SUBS * s + m + 1)
                            gp.indirect_dma_start(out=out_rows, in_=finished[m][k][:, :], in_offset=None,
                                                  out_offset=bass.IndirectOffsetOnAxis(ap=scatter_ids[m][k][:, 0:1], axis=0),
                                                  bounds_check=TOKENS - 1, oob_is_err=False).then_inc(scattered[m][k], 16)

                        if v := visit(i, u, 0, SLOTS):
                            s, use, k = v
                            wait_alone(gp, finished_ready, SUBS * (s - 2) + m + 1)
                            gather(residual[m][k][:, :], residual_rows, gather_ids[m][k]).then_inc(residual_in[m][k], 16)

                run_steps(gp, SLOTS, LAG3, step)
                for k in range(2):
                    for m in range(SUBS):
                        gp.wait_ge(scattered[m][k], 16 * ((SLOTS + 1 - k) // 2))

            @block.tensor
            def _(pe):
                flat = onehot[:, :, :].rearrange("p b e -> p (b e)")
                pe.wait_ge(onehot_ready, 1)
                nc.tensor.matmul(count_ps[:, 0:B * NE], ones[:, :], flat, start=True, stop=True).then_inc(ranks_ready, 1)
                nc.tensor.matmul(rank_ps[:, 0:B * NE], before[:, :], flat, start=True, stop=True).then_inc(ranks_ready, 1)
                for b in range(B):
                    if b % GB == 0:
                        pe.wait_ge(lanes_ready, b // GB + 1)
                        pe.wait_ge(weights_ready, b // GB + 1)
                    last = nc.tensor.matmul(table_ps[:, 0:VALUES * BLOCKS], in_lane[b // (B // 2)][:, b % (B // 2), :],
                                            in_block[:, b, :, :].rearrange("p a n -> p (a n)"),
                                            start=(b == 0), stop=(b == B - 1))
                last.then_inc(table_ready, 1)

                def down(s, k, m, chunks):
                    if chunks[0] == 0:
                        wait(pe, plus_b2_ready, SUBS * (s - 1) + m + 1)
                    for c in chunks:
                        if m == 0 and c % 2 == 0:
                            wait(pe, hidden_lo_ready, PAIRS * s + c // 2 + 1)
                        block_m = slice(m * P, (m + 1) * P)
                        last = split_products(down_ps[m][:, 0:E], hidden_hi[k][:, c, block_m], hidden_lo[k][:, c, block_m],
                                              w2_hi[k][:, c, :], w2_lo[k][:, c, :], c == 0, c == HC - 1)
                    if c == HC - 1:
                        last.then_inc(down_ready, 1)

                def step(i, u):
                    if v := visit(i, u, 2, SLOTS):
                        s, use, k = v
                        wait(pe, slotT_lo_ready, s + 1)
                        wait(pe, w1_lo_ready, PAIRS * (s + 1))
                        for c in range(HC):
                            if c % 2 == 0:
                                wait(pe, silu_done, PAIRS * (s - 1) + c // 2 + 1)
                            for kc in range(KC):
                                chunk = slice(c * P, (c + 1) * P)
                                last = split_products(wide[:, c // 2, (c % 2) * SLOT_TOKENS:(c % 2 + 1) * SLOT_TOKENS],
                                                      w1_hi[k][:, kc, chunk], w1_lo[k][:, kc, chunk],
                                                      slotT_hi[k][:, kc, :], slotT_lo[k][:, kc, :], kc == 0, kc == KC - 1)
                            if c % 2:
                                last.then_inc(up_ready, 1)
                        wait(pe, w2_lo_ready, W2_PARTS * (s + 1))
                        down(s, k, 0, range(0, HC - 2))
                        down(s, k, 1, range(0, HC // 2))
                    if v := visit(i, u, 1, SLOTS):
                        s, use, k = v
                        wait(pe, slotT_lo_ready, s)
                        for m in range(SUBS):
                            pe.wait_ge(normed_in[m][k], 16 * use + 16)
                            for c in range(KC):
                                last = nc.tensor.transpose(slot_ps[:, c * SLOT_TOKENS + m * P:c * SLOT_TOKENS + (m + 1) * P],
                                                           normed[m][k][:, c * P:(c + 1) * P], ident[:, :])
                        last.then_inc(slotT_ready, 1)
                    if v := visit(i, u, 2, SLOTS):
                        s, use, k = v
                        down(s, k, 0, range(HC - 2, HC))
                        down(s, k, 1, range(HC // 2, HC))

                run_steps(pe, SLOTS, LAG3, step)

            @block.scalar
            def _(act):
                act.wait_ge(below_ready, 1)
                nc.scalar.activation(expd[:, :, :], below[:, :, :], ACT.Exp).then_inc(exp_ready, 1)
                nc.scalar.preload_act_table(ACT.Silu)

                def step(i, u):
                    if v := visit(i, u, 2, SLOTS):
                        s, use, k = v
                        wait(act, picks_ready, s + 1)
                        wait(act, hidden_lo_ready, PAIRS * s)
                        wait(act, down_ready, SUBS * (s - 1))
                        for p in range(PAIRS):
                            wait(act, up_ready, PAIRS * s + p + 1)
                            for c in (2 * p, 2 * p + 1):
                                last = nc.scalar.activation(hidden[:, c, :],
                                                            wide[:, p, (c % 2) * SLOT_TOKENS:(c % 2 + 1) * SLOT_TOKENS],
                                                            ACT.Silu, bias=b1_cols[k][:, c:c + 1])
                            last.then_inc(silu_done, 1)
                            wait(act, silu_done, PAIRS * s + p + 1)
                            nc.scalar.copy(hidden_hi[k][:, 2 * p:2 * p + 2, :],
                                           hidden[:, 2 * p:2 * p + 2, :]).then_inc(hidden_hi_ready, 1)
                    if v := visit(i, u, 1, SLOTS):
                        s, use, k = v
                        act.wait_ge(w2_loaded[k], 16 * use + 16)
                        wait(act, down_ready, SUBS * (s - 1))
                        nc.scalar.copy(w2_hi[k][:, :, :], w2_in[k][:, :, :]).then_inc(w2_hi_ready, 1)
                    if v := visit(i, u, 0, SLOTS):
                        s, use, k = v
                        act.wait_ge(w1_loaded[k], 16 * use + 16)
                        wait(act, up_ready, PAIRS * (s - 1))
                        nc.scalar.copy(w1_hi[k][:, :, :], w1_in[k][:, :, :]).then_inc(w1_hi_ready, 1)

                run_steps(act, SLOTS, LAG3, step)

            @block.vector
            def _(dve):
                done = [0]

                def after(ins):
                    done[0] += 1
                    ins.then_inc(r_chain, 1)
                    dve.wait_ge(r_chain, done[0])

                def by_expert(a):
                    return a.unsqueeze(2).broadcast_to([P, B, NE])

                dve.wait_ge(iotas, 6)
                after(nc.vector.tensor_reduce(out=best[:, :], in_=logits[:, :, :], axis=AX.X, op=ALU.max))
                nc.vector.tensor_tensor(below[:, :, :], logits[:, :, :], by_expert(best[:, :]),
                                        ALU.subtract).then_inc(below_ready, 1)
                dve.wait_ge(below_ready, 1)
                after(nc.vector.tensor_scalar(is_best[:, :, :], below[:, :, :], 0.0, None, ALU.is_ge))
                after(nc.vector.tensor_tensor(is_best[:, :, :], is_best[:, :, :],
                                              expert_rank[:, :].unsqueeze(1).broadcast_to([P, B, NE]), ALU.mult))
                after(nc.vector.tensor_reduce(out=chosen[:, :], in_=is_best[:, :, :], axis=AX.X, op=ALU.max))
                nc.vector.tensor_tensor(onehot[:, :, :], by_expert(chosen[:, :]),
                                        expert_rank[:, :].unsqueeze(1).broadcast_to([P, B, NE]),
                                        ALU.is_equal).then_inc(onehot_ready, 1)
                dve.wait_ge(exp_ready, 1)
                after(nc.vector.tensor_reduce(out=total[:, :], in_=expd[:, :, :], axis=AX.X, op=ALU.add))
                after(nc.vector.reciprocal(weight[:, :], total[:, :]))
                after(nc.vector.tensor_copy(weight_hi[:, :], weight[:, :]))
                after(low_part(weight_lo[:, :], weight[:, :], weight_hi[:, :]))
                dve.wait_ge(ranks_ready, 1)
                after(nc.vector.tensor_copy(counts[:, :, :], count_ps[:, 0:B * NE].rearrange("p (b e) -> p e b", e=NE)))
                flat = "p e b -> p (e b)"
                after(nc.vector.tensor_tensor_scan(out=running[:, :, :].rearrange(flat), data0=ones[:, 0:1].broadcast_to([P, NE * B]),
                                                   data1=counts[:, :, :].rearrange(flat), initial=0.0,
                                                   op0=ALU.mult, op1=ALU.add))
                after(nc.vector.tensor_tensor(earlier[:, :, :], running[:, :, :], counts[:, :, :], ALU.subtract))
                after(nc.vector.tensor_tensor(n_tokens[:, :], running[:, :, B - 1], earlier[:, :, 0], ALU.subtract))
                after(nc.vector.tensor_tensor(more_than[:, :, :], n_tokens[:, :].unsqueeze(2).broadcast_to([P, NE, FULL_SLOTS]),
                                              slot_fill[:, :].unsqueeze(1).broadcast_to([P, NE, FULL_SLOTS]), ALU.is_gt))
                after(nc.vector.tensor_reduce(out=n_slots[:, :], in_=more_than[:, :, :], axis=AX.X, op=ALU.add))
                after(nc.vector.tensor_tensor_scan(out=slot_end[:, :], data0=ones[:, 0:NE], data1=n_slots[:, :],
                                                   initial=0.0, op0=ALU.mult, op1=ALU.add))
                after(nc.vector.tensor_tensor(past[:, :, :], slot_no[0:1, :].unsqueeze(2).broadcast_to([1, SLOTS, NE]),
                                              slot_end[0:1, :].unsqueeze(1).broadcast_to([1, SLOTS, NE]), ALU.is_ge))
                after(nc.vector.tensor_reduce(out=slot_expert_f[:, :], in_=past[:, :, :], axis=AX.X, op=ALU.add))
                after(nc.vector.tensor_scalar_min(slot_expert_f[:, :], slot_expert_f[:, :], float(NE - 1)))
                nc.vector.tensor_copy(slot_expert[:, :], slot_expert_f[:, :]).then_inc(slot_expert_ready, 1)
                after(nc.vector.tensor_tensor(first_row[:, :], slot_end[:, :], n_slots[:, :], ALU.subtract))
                after(nc.vector.scalar_tensor_tensor(out=first_row[:, :], in0=first_row[:, :], scalar=float(SLOT_TOKENS),
                                                     in1=earlier[:, :, 0], op0=ALU.mult, op1=ALU.subtract))
                dve.wait_ge(ranks_ready, 2)
                after(nc.vector.tensor_tensor(place[:, :, :], rank_ps[:, 0:B * NE].rearrange("p (b e) -> p b e", e=NE),
                                              earlier[:, :, :].rearrange("p e b -> p b e"), ALU.add))
                after(nc.vector.tensor_tensor(place[:, :, :], place[:, :, :],
                                              first_row[:, :].unsqueeze(1).broadcast_to([P, B, NE]), ALU.add))
                after(nc.vector.tensor_tensor(picked[:, :, :], place[:, :, :], onehot[:, :, :], ALU.mult))
                after(nc.vector.tensor_reduce(out=position[:, :], in_=picked[:, :, :], axis=AX.X, op=ALU.add))
                after(nc.vector.tensor_copy(position_i[:, :], position[:, :]))
                nc.vector.tensor_scalar(lane_i[:, :], position_i[:, :], P - 1, None, ALU.bitwise_and).then_inc(r_chain, 1)
                done[0] += 1
                after(nc.vector.tensor_scalar(block_i[:, :], position_i[:, :], P.bit_length() - 1, None,
                                              ALU.logical_shift_right))
                nc.vector.tensor_copy(lane_f[:, :], lane_i[:, :]).then_inc(r_chain, 1)
                done[0] += 1
                after(nc.vector.tensor_copy(block_f[:, :], block_i[:, :]))
                for g in range(GROUPS):
                    s = slice(g * GB, (g + 1) * GB)
                    wide_shape = [P, GB, BLOCKS]
                    nc.vector.tensor_tensor(at_block[:, s, :], block_no[:, :].unsqueeze(1).broadcast_to(wide_shape),
                                            block_f[:, s].unsqueeze(2).broadcast_to(wide_shape),
                                            ALU.is_equal).then_inc(at_block_ready, 1)
                    nc.vector.tensor_tensor(in_lane[g // 2][:, g % 2 * GB:(g % 2 + 1) * GB, :],
                                            lane_no[:, :].unsqueeze(1).broadcast_to([P, GB, P]),
                                            lane_f[:, s].unsqueeze(2).broadcast_to([P, GB, P]), ALU.is_equal)
                    dve.wait_ge(at_block_ready, g + 1)
                    nc.vector.tensor_tensor(in_block[:, s, 0, :], at_block[:, s, :],
                                            token1[:, s].unsqueeze(2).broadcast_to(wide_shape),
                                            ALU.mult).then_inc(lanes_ready, 1)
                dve.wait_ge(table_ready, 1)
                token_sum, hi_sum, lo_sum = (table_ps[:, n * BLOCKS:(n + 1) * BLOCKS] for n in range(VALUES))
                after(nc.vector.tensor_scalar(padding[:, :], token_sum, 0.5, float(2 * TOKENS), ALU.is_lt, ALU.mult))
                after(nc.vector.scalar_tensor_tensor(out=row_id_f[:, :], in0=token_sum, scalar=-1.0,
                                                     in1=padding[:, :], op0=ALU.add, op1=ALU.add))
                nc.vector.tensor_copy(row_id[:, :], row_id_f[:, :]).then_inc(row_table_ready, 1)
                after(nc.vector.tensor_copy(weight_sum[:, :], lo_sum))
                after(nc.vector.tensor_tensor(row_weight[:, :], hi_sum, weight_sum[:, :], ALU.add))

                def finish(s, use, k, m):
                    wait(dve, down_ready, SUBS * s + m + 1)
                    nc.vector.tensor_tensor(plus_b2[m][k][:, :], down_ps[m][:, 0:E], b2_rows[k][:, :],
                                            ALU.add).then_inc(plus_b2_ready, 1)
                    wait(dve, plus_b2_ready, SUBS * s + m + 1)
                    dve.wait_ge(residual_in[m][k], 16 * use + 16)
                    if not isinstance(use, int) or use > 0:
                        dve.wait_ge(scattered[m][k], 16 * use)
                    nc.vector.scalar_tensor_tensor(out=finished[m][k][:, :], in0=plus_b2[m][k][:, :],
                                                   scalar=weights[k][:, m:m + 1], in1=residual[m][k][:, :],
                                                   op0=ALU.mult, op1=ALU.add).then_inc(finished_ready, 1)

                def w2_low(s, k, part):
                    cs = slice(part * W2_C, (part + 1) * W2_C)
                    low_part(w2_lo[k][:, cs, :], w2_in[k][:, cs, :], w2_hi[k][:, cs, :]).then_inc(w2_lo_ready, 1)

                def step(i, u):
                    current, following = visit(i, u, 2, SLOTS), visit(i, u, 1, SLOTS)
                    for p in range(PAIRS):
                        if current:
                            s, use, k = current
                            wait(dve, hidden_hi_ready, PAIRS * s + p + 1)
                            wait(dve, down_ready, SUBS * (s - 1))
                            low_part(hidden_lo[k][:, 2 * p:2 * p + 2, :], hidden[:, 2 * p:2 * p + 2, :],
                                     hidden_hi[k][:, 2 * p:2 * p + 2, :]).then_inc(hidden_lo_ready, 1)
                        if following:
                            s, use, k = following
                            wait(dve, w1_hi_ready, s + 1)
                            wait(dve, up_ready, PAIRS * (s - 1))
                            kc, n = divmod(p * W1_N, HID)
                            low_part(w1_lo[k][:, kc, n:n + W1_N], w1_in[k][:, kc, n:n + W1_N],
                                     w1_hi[k][:, kc, n:n + W1_N]).then_inc(w1_lo_ready, 1)
                    if following:
                        s, use, k = following
                        e = dve.value_load(slot_expert[0:1, bass.ds(s, 1)], min_val=0, max_val=NE - 1)
                        wait(dve, silu_done, PAIRS * (s - 1))
                        wait(dve, finished_ready, SUBS * (s - 1))
                        nc.vector.tensor_copy(b1_cols[k][:, :], b1T[:, bass.ds(e * HC, HC)])
                        nc.vector.tensor_copy(weights[k][:, :], row_weight[:, bass.ds(SUBS * s, SUBS)]).then_inc(picks_ready, 1)
                        wait(dve, slotT_ready, s + 1)
                        wait(dve, up_ready, PAIRS * (s - 1))
                        by_chunk = slot_ps[:, :].rearrange("p (c s) -> p c s", c=KC)
                        nc.vector.tensor_copy(slotT_hi[k][:, :, :], by_chunk).then_inc(slotT_hi_ready, 1)
                        wait(dve, slotT_hi_ready, s + 1)
                        low_part(slotT_lo[k][:, :, :], by_chunk, slotT_hi[k][:, :, :]).then_inc(slotT_lo_ready, 1)
                    if current:
                        s, use, k = current
                        wait(dve, picks_ready, s + 1)
                        dve.wait_ge(b2_loaded[k], 16 * use + 16)
                        finish(s, use, k, 0)
                    if following:
                        s, use, k = following
                        wait(dve, w2_hi_ready, s + 1)
                        wait(dve, down_ready, SUBS * (s - 1))
                        w2_low(s, k, 0)
                    if current:
                        s, use, k = current
                        finish(s, use, k, 1)
                    if following:
                        s, use, k = following
                        w2_low(s, k, 1)

                run_steps(dve, SLOTS, LAG3, step)


_INS = ["x", "L0_tok_W", "L0_tok_b", "L0_attn_Wq", "L0_attn_bq", "L0_attn_Wk", "L0_attn_bk", "L0_attn_Wv",
        "L0_attn_bv", "L0_attn_Wo", "L0_attn_bo", "L0_ffn_Wg", "L0_ffn_bg", "L0_ffn_W1", "L0_ffn_b1",
        "L0_ffn_W2", "L0_ffn_b2"]


def kernel(**inputs):
    import numpy as np
    import concourse.bacc as bacc
    from concourse.bass_utils import run_bass_kernel_spmd

    nc = bacc.Bacc("TRN2", target_bir_lowering=False, num_devices=1)
    arrays, args = {}, []
    for name in _INS:
        a = np.ascontiguousarray(inputs[name])
        arrays[f"in_{name}"] = a
        args.append(nc.dram_tensor(f"in_{name}", a.shape, mybir.dt.from_np(a.dtype), kind="ExternalInput").ap())
    batch, _, tokens, _ = arrays["in_x"].shape
    embed = arrays["in_L0_tok_W"].shape[0]
    out = nc.dram_tensor("out", (batch, tokens, embed), mybir.dt.float32, kind="ExternalOutput").ap()
    tower(nc, *args, out)
    return run_bass_kernel_spmd(nc, [arrays], core_ids=[0]).results[0]["out"]
```
